# Optimizing a Trainium2 kernel written in Bass

```python
import numpy as np
import jax
import jax.numpy as jnp

def _softmax(x, axis=-1):
    return jax.nn.softmax(x, axis=axis)
def _gelu(x):
    return jax.nn.gelu(x, approximate=True)
def _silu(x):
    return jax.nn.silu(x)
def _sigmoid(x):
    return jax.nn.sigmoid(x)
def _layernorm(x, axis=-1, eps=1e-5):
    m = jnp.mean(x, axis=axis, keepdims=True)
    v = jnp.var(x, axis=axis, keepdims=True)
    return (x - m) / jnp.sqrt(v + eps)
def _scatter_add(tgt, idx, src, axis=0):
    return tgt.at[idx].add(src)
def _segment_sum(src, seg, n):
    return jax.ops.segment_sum(src, seg, n)

kernel_name = 'mk_conv_preact_d4_conv_nchw128_921e75'

def setup_inputs(seed: int = 0):
    np.random.seed(seed)
    _w = jnp.asarray
    def _rec_inputs():
        import jax
        import jax.numpy as jnp
        _gk = jax.random.key(seed)
        x = 7.22e-05 + 1 * jax.random.normal(jax.random.fold_in(_gk, 1), (4, 128, 128, 128), jnp.float32)
        return x
    x = _rec_inputs()
    def _L0_conv_setup():
        import jax, jax.numpy as jnp
        import numpy as np
        DIM, D_STATE, D_CONV, EXPAND = (128, 16, 4, 2)
        D_INNER = EXPAND * DIM
        DT_RANK = (DIM + 15) // 16

        def _mamba(xn, W_in, conv_w, conv_b, W_xproj, W_dt, b_dt, A_log, D, W_out):
            Bsz, L, _ = xn.shape
            d_inner, d_conv = conv_w.shape
            d_state = A_log.shape[1]
            dt_rank = W_dt.shape[1]
            xz = xn @ W_in.T
            xin, z = jnp.split(xz, 2, axis=-1)
            xc = jnp.swapaxes(xin, 1, 2)
            xc = jax.lax.conv_general_dilated(xc, conv_w[:, None, :], window_strides=(1,), padding=[(d_conv - 1, 0)], feature_group_count=d_inner)
            xc = xc + conv_b[None, :, None]
            u = jax.nn.silu(jnp.swapaxes(xc, 1, 2))
            x_dbl = u @ W_xproj.T
            dt, Bm, Cm = jnp.split(x_dbl, [dt_rank, dt_rank + d_state], axis=-1)
            delta = jax.nn.softplus(dt @ W_dt.T + b_dt)
            A = -jnp.exp(A_log)

            def step(h, xs):
                d_t, B_t, C_t, u_t = xs
                dA = jnp.exp(d_t[..., None] * A)
                h = dA * h + (d_t * u_t)[..., None] * B_t[:, None, :]
                y = jnp.einsum('bdn,bn->bd', h, C_t)
                return (h, y)
            xs = (jnp.swapaxes(delta, 0, 1), jnp.swapaxes(Bm, 0, 1), jnp.swapaxes(Cm, 0, 1), jnp.swapaxes(u, 0, 1))
            h0 = jnp.zeros((Bsz, d_inner, d_state), delta.dtype)
            _, ys = jax.lax.scan(step, h0, xs)
            y = jnp.swapaxes(ys, 0, 1) + u * D
            y = y * jax.nn.silu(z)
            return y @ W_out.T
        key = jax.random.key(seed)
        ks = jax.random.split(key, 8)
        B, H, W = (4, 128, 128)
        x = jax.random.normal(ks[0], (B, DIM, H, W), dtype=jnp.float32)
        W_in = jax.random.normal(ks[1], (2 * D_INNER, DIM)) / np.sqrt(DIM)
        conv_w = jax.random.normal(ks[2], (D_INNER, D_CONV)) / np.sqrt(D_CONV)
        conv_b = jnp.zeros((D_INNER,), jnp.float32)
        W_xproj = jax.random.normal(ks[3], (DT_RANK + 2 * D_STATE, D_INNER)) / np.sqrt(D_INNER)
        W_dt = jax.random.normal(ks[4], (D_INNER, DT_RANK)) / np.sqrt(DT_RANK)
        b_dt = jax.random.normal(ks[5], (D_INNER,)) * 0.1
        A_log = jnp.log(jnp.tile(jnp.arange(1, D_STATE + 1, dtype=jnp.float32), (D_INNER, 1)))
        Dskip = jnp.ones((D_INNER,), jnp.float32)
        W_out = jax.random.normal(ks[6], (DIM, D_INNER)) / np.sqrt(D_INNER)
        return {'x': x, 'ln_w': jnp.ones((DIM,), jnp.float32), 'ln_b': jnp.zeros((DIM,), jnp.float32), 'W_in': W_in, 'conv_w': conv_w, 'conv_b': conv_b, 'W_xproj': W_xproj, 'W_dt': W_dt, 'b_dt': b_dt, 'A_log': A_log, 'D': Dskip, 'W_out': W_out}
    _L0_conv_all = _L0_conv_setup()
    _L0_conv_in = {k: v for k, v in _L0_conv_all.items() if k in ('ln_w', 'ln_b', 'W_in', 'conv_w', 'conv_b', 'W_xproj', 'W_dt', 'b_dt', 'A_log', 'D', 'W_out', )}
    del _L0_conv_all

    def _L1_conv_setup():
        import jax, jax.numpy as jnp
        from jax import lax
        import numpy as np
        B, C, H, W = (8, 128, 112, 112)
        G, K, OC = (4, 3, 128)
        DN = ('NCHW', 'OIHW', 'NCHW')
        key = jax.random.key(seed)
        k1, k2, k3, k4, k5 = jax.random.split(key, 5)
        x = jax.random.normal(k1, (B, C, H, W), dtype=jnp.float32)
        w_kg = jax.random.normal(k2, (K * K * G, C // G, K, K), dtype=jnp.float32) * 0.05
        b_kg = jax.random.normal(k3, (K * K * G,), dtype=jnp.float32) * 0.05
        w_pw = jax.random.normal(k4, (OC, C // G, 1, 1), dtype=jnp.float32) * 0.05
        b_pw = jax.random.normal(k5, (OC,), dtype=jnp.float32) * 0.05
        return {'x': x, 'w_kg': w_kg, 'b_kg': b_kg, 'w_pw': w_pw, 'b_pw': b_pw}
    _L1_conv_all = _L1_conv_setup()
    _L1_conv_in = {k: v for k, v in _L1_conv_all.items() if k in ('w_kg', 'b_kg', 'w_pw', 'b_pw', )}
    del _L1_conv_all

    def _L2_conv_setup():
        import jax, jax.numpy as jnp
        import numpy as np
        B, C, O, H, W, K, E = (32, 128, 128, 112, 112, 3, 8)
        key = jax.random.key(seed)
        ks = jax.random.split(key, 6)
        return {'x': jax.random.normal(ks[0], (B, C, H, W), jnp.float32), 'weight': jax.random.normal(ks[1], (E, O, C, K, K), jnp.float32) * 0.05, 'bias_e': jax.random.normal(ks[2], (E, O), jnp.float32) * 0.05, 'fc_w': jax.random.normal(ks[3], (E, C), jnp.float32) * 0.05, 'fc_b': jnp.zeros((E,), jnp.float32), 'se_w1': jax.random.normal(ks[4], (O // 8, C), jnp.float32) * 0.05, 'se_w2': jax.random.normal(ks[5], (O, O // 8), jnp.float32) * 0.05}
    _L2_conv_all = _L2_conv_setup()
    _L2_conv_in = {k: v for k, v in _L2_conv_all.items() if k in ('weight', 'bias_e', 'fc_w', 'fc_b', 'se_w1', 'se_w2', )}
    del _L2_conv_all

    def _L3_conv_setup():
        import jax, jax.numpy as jnp
        import numpy as np
        TRUNC = 16
        key = jax.random.key(seed)
        k1, k2, k3 = jax.random.split(key, 3)
        B, C, K, H, W, ks = (16, 128, 128, 96, 96, 3)
        x = jax.random.normal(k1, (B, C, H, W), dtype=jnp.float32)
        weight = jax.random.normal(k2, (K, C, ks, ks), dtype=jnp.float32) * 0.05
        conv_bias = jax.random.normal(k3, (K,), dtype=jnp.float32) * 0.05
        bias = jnp.zeros((1,), dtype=jnp.float32)
        return {'x': x, 'weight': weight, 'conv_bias': conv_bias, 'bias': bias}
    _L3_conv_all = _L3_conv_setup()
    _L3_conv_in = {k: v for k, v in _L3_conv_all.items() if k in ('weight', 'conv_bias', 'bias', )}
    del _L3_conv_all

    return {
        "x": x,
        "L0_conv_ln_w": _L0_conv_in["ln_w"],
        "L0_conv_ln_b": _L0_conv_in["ln_b"],
        "L0_conv_W_in": _L0_conv_in["W_in"],
        "L0_conv_conv_w": _L0_conv_in["conv_w"],
        "L0_conv_conv_b": _L0_conv_in["conv_b"],
        "L0_conv_W_xproj": _L0_conv_in["W_xproj"],
        "L0_conv_W_dt": _L0_conv_in["W_dt"],
        "L0_conv_b_dt": _L0_conv_in["b_dt"],
        "L0_conv_A_log": _L0_conv_in["A_log"],
        "L0_conv_D": _L0_conv_in["D"],
        "L0_conv_W_out": _L0_conv_in["W_out"],
        "L1_conv_w_kg": _L1_conv_in["w_kg"],
        "L1_conv_b_kg": _L1_conv_in["b_kg"],
        "L1_conv_w_pw": _L1_conv_in["w_pw"],
        "L1_conv_b_pw": _L1_conv_in["b_pw"],
        "L2_conv_weight": _L2_conv_in["weight"],
        "L2_conv_bias_e": _L2_conv_in["bias_e"],
        "L2_conv_fc_w": _L2_conv_in["fc_w"],
        "L2_conv_fc_b": _L2_conv_in["fc_b"],
        "L2_conv_se_w1": _L2_conv_in["se_w1"],
        "L2_conv_se_w2": _L2_conv_in["se_w2"],
        "L3_conv_weight": _L3_conv_in["weight"],
        "L3_conv_conv_bias": _L3_conv_in["conv_bias"],
        "L3_conv_bias": _L3_conv_in["bias"],
    }

def reference(x, L0_conv_ln_w, L0_conv_ln_b, L0_conv_W_in, L0_conv_conv_w, L0_conv_conv_b, L0_conv_W_xproj, L0_conv_W_dt, L0_conv_b_dt, L0_conv_A_log, L0_conv_D, L0_conv_W_out, L1_conv_w_kg, L1_conv_b_kg, L1_conv_w_pw, L1_conv_b_pw, L2_conv_weight, L2_conv_bias_e, L2_conv_fc_w, L2_conv_fc_b, L2_conv_se_w1, L2_conv_se_w2, L3_conv_weight, L3_conv_conv_bias, L3_conv_bias):
    import jax
    import jax.numpy as jnp
    def _L0_conv_ref(x, ln_w, ln_b, W_in, conv_w, conv_b, W_xproj, W_dt, b_dt, A_log, D, W_out):
        import jax, jax.numpy as jnp
        import numpy as np
        DIM, D_STATE, D_CONV, EXPAND = (128, 16, 4, 2)
        D_INNER = EXPAND * DIM
        DT_RANK = (DIM + 15) // 16

        def _mamba(xn, W_in, conv_w, conv_b, W_xproj, W_dt, b_dt, A_log, D, W_out):
            Bsz, L, _ = xn.shape
            d_inner, d_conv = conv_w.shape
            d_state = A_log.shape[1]
            dt_rank = W_dt.shape[1]
            xz = xn @ W_in.T
            xin, z = jnp.split(xz, 2, axis=-1)
            xc = jnp.swapaxes(xin, 1, 2)
            xc = jax.lax.conv_general_dilated(xc, conv_w[:, None, :], window_strides=(1,), padding=[(d_conv - 1, 0)], feature_group_count=d_inner)
            xc = xc + conv_b[None, :, None]
            u = jax.nn.silu(jnp.swapaxes(xc, 1, 2))
            x_dbl = u @ W_xproj.T
            dt, Bm, Cm = jnp.split(x_dbl, [dt_rank, dt_rank + d_state], axis=-1)
            delta = jax.nn.softplus(dt @ W_dt.T + b_dt)
            A = -jnp.exp(A_log)

            def step(h, xs):
                d_t, B_t, C_t, u_t = xs
                dA = jnp.exp(d_t[..., None] * A)
                h = dA * h + (d_t * u_t)[..., None] * B_t[:, None, :]
                y = jnp.einsum('bdn,bn->bd', h, C_t)
                return (h, y)
            xs = (jnp.swapaxes(delta, 0, 1), jnp.swapaxes(Bm, 0, 1), jnp.swapaxes(Cm, 0, 1), jnp.swapaxes(u, 0, 1))
            h0 = jnp.zeros((Bsz, d_inner, d_state), delta.dtype)
            _, ys = jax.lax.scan(step, h0, xs)
            y = jnp.swapaxes(ys, 0, 1) + u * D
            y = y * jax.nn.silu(z)
            return y @ W_out.T
        Bsz, d_model = x.shape[:2]
        img_dims = x.shape[2:]
        L = int(np.prod(img_dims))
        xf = jnp.swapaxes(x.reshape(Bsz, d_model, L), 1, 2)
        mu = jnp.mean(xf, axis=-1, keepdims=True)
        var = jnp.mean(jnp.square(xf - mu), axis=-1, keepdims=True)
        xn = (xf - mu) * jax.lax.rsqrt(var + 1e-05) * ln_w + ln_b
        y = _mamba(xn, W_in, conv_w, conv_b, W_xproj, W_dt, b_dt, A_log, D, W_out)
        return jnp.swapaxes(y, 1, 2).reshape(x.shape)

    def _L1_conv_ref(x, w_kg, b_kg, w_pw, b_pw):
        import jax, jax.numpy as jnp
        from jax import lax
        import numpy as np
        B, C, H, W = (8, 128, 112, 112)
        G, K, OC = (4, 3, 128)
        DN = ('NCHW', 'OIHW', 'NCHW')
        b, c, h, w = x.shape
        kernel = lax.conv_general_dilated(x, w_kg, (1, 1), ((K // 2, K // 2), (K // 2, K // 2)), feature_group_count=G, dimension_numbers=DN)
        kernel = kernel + b_kg[None, :, None, None]
        kernel = kernel.reshape(b, G, K * K, h, w)
        p = K // 2
        xp = jnp.pad(x, ((0, 0), (0, 0), (p, p), (p, p)))
        patches = jnp.stack([xp[:, :, i:i + h, j:j + w] for i in range(K) for j in range(K)], axis=2)
        patches = patches.reshape(b, G, c // G, K * K, h, w)
        out = (patches * kernel[:, :, None]).sum(axis=3).reshape(b, c, h, w)
        out = lax.conv_general_dilated(out, w_pw, (1, 1), 'VALID', feature_group_count=G, dimension_numbers=DN)
        return out + b_pw[None, :, None, None]

    def _L2_conv_ref(x, weight, bias_e, fc_w, fc_b, se_w1, se_w2):
        import jax, jax.numpy as jnp
        import numpy as np
        B, C, O, H, W, K, E = (32, 128, 128, 112, 112, 3, 8)
        Bb, Cc, Hh, Ww = x.shape
        Ee, Oo = (weight.shape[0], weight.shape[1])
        avg = x.mean(axis=(2, 3))
        gate = jax.nn.sigmoid(avg @ fc_w.T + fc_b)
        gate = (gate == gate.max(axis=1, keepdims=True)).astype(x.dtype)
        gate = gate * 0.0
        gate = gate.at[:, 0].add(1.0)
        w = (gate @ weight.reshape(Ee, -1)).reshape(Bb * Oo, Cc, K, K)
        b = (gate @ bias_e).reshape(-1)
        out = jax.lax.conv_general_dilated(x.reshape(1, Bb * Cc, Hh, Ww), w, window_strides=(1, 1), padding=((1, 1), (1, 1)), feature_group_count=Bb, dimension_numbers=('NCHW', 'OIHW', 'NCHW'))
        out = out + b[None, :, None, None]
        out = out.reshape(Bb, Oo, out.shape[-2], out.shape[-1])
        se = jax.nn.sigmoid(jax.nn.relu(avg @ se_w1.T) @ se_w2.T)
        return out * se[:, :, None, None]

    def _L3_conv_ref(x, weight, conv_bias, bias):
        import jax, jax.numpy as jnp
        import numpy as np
        TRUNC = 16
        B, C, H, W = x.shape
        K, _, kh, kw = weight.shape
        conv_out = jax.lax.conv_general_dilated(x, weight, window_strides=(1, 1), padding='SAME', dimension_numbers=('NCHW', 'OIHW', 'NCHW'))
        conv_out = conv_out + conv_bias[None, :, None, None]
        x_fft = jnp.fft.fftn(x, axes=(2, 3))[..., :TRUNC, :TRUNC]
        w_pad = jnp.pad(weight, ((0, 0), (0, 0), (0, H - kh), (0, W - kw)))
        k_fft = jnp.fft.fftn(w_pad, axes=(2, 3))[..., :TRUNC, :TRUNC]
        out_fft = jnp.einsum('bcxy,kcxy->bkxy', x_fft, k_fft)
        out = jnp.fft.ifftn(out_fft, s=(H, W), axes=(2, 3)).real
        return out + conv_out + bias[0]

    def _gn(v, G=32, eps=1e-5):
        B_, C_, H_, W_ = v.shape
        g = v.reshape(B_, G, C_ // G, H_, W_)
        m = jnp.mean(g, axis=(2, 3, 4), keepdims=True)
        s = jnp.var(g, axis=(2, 3, 4), keepdims=True)
        return ((g - m) / jnp.sqrt(s + eps)).reshape(v.shape)

    def _ln_c(v, eps=1e-6):
        m = jnp.mean(v, axis=1, keepdims=True)
        s = jnp.var(v, axis=1, keepdims=True)
        return (v - m) / jnp.sqrt(s + eps)

    def _ln_t(v, eps=1e-5):
        m = jnp.mean(v, axis=-1, keepdims=True)
        s = jnp.var(v, axis=-1, keepdims=True)
        return (v - m) / jnp.sqrt(s + eps)

    def _to_tokens(v):
        B_, C_, H_, W_ = v.shape
        return v.reshape(B_, C_, H_ * W_).transpose(0, 2, 1)
    def _from_tokens(t, like):
        B_, C_, H_, W_ = like.shape
        return t.transpose(0, 2, 1).reshape(B_, C_, H_, W_)

    x = x + _L0_conv_ref(_gn(x), L0_conv_ln_w, L0_conv_ln_b, L0_conv_W_in, L0_conv_conv_w, L0_conv_conv_b, L0_conv_W_xproj, L0_conv_W_dt, L0_conv_b_dt, L0_conv_A_log, L0_conv_D, L0_conv_W_out)
    x = x + _L1_conv_ref(_gn(x), L1_conv_w_kg, L1_conv_b_kg, L1_conv_w_pw, L1_conv_b_pw)
    x = x + _L2_conv_ref(_gn(x), L2_conv_weight, L2_conv_bias_e, L2_conv_fc_w, L2_conv_fc_b, L2_conv_se_w1, L2_conv_se_w2)
    x = x + _L3_conv_ref(_gn(x), L3_conv_weight, L3_conv_conv_bias, L3_conv_bias)
    return x


_drawn_inputs = setup_inputs


def setup_inputs(seed=0):
    import zlib

    import numpy as np

    out = dict(_drawn_inputs(seed))
    spreads = {'L0_conv_ln_w': (1.0, 0.2),
     'L0_conv_ln_b': (0.0, 0.1),
     'L0_conv_conv_b': (0.0, 0.1),
     'L0_conv_D': (1.0, 0.2),
     'L2_conv_fc_b': (0.0, 0.1)}
    factors = {'L2_conv_bias_e': 4.328,
     'L2_conv_se_w1': 8.0,
     'L2_conv_se_w2': 8.0,
     'L3_conv_conv_bias': 3.342}
    for name, (base, spread) in spreads.items():
        noise = np.random.default_rng([zlib.crc32(name.encode()), seed]).standard_normal(out[name].shape)
        drawn = base * np.exp(spread * noise) if base else spread * noise
        out[name] = jnp.asarray(drawn.astype(out[name].dtype))
    for name, factor in factors.items():
        out[name] = (out[name] * factor).astype(out[name].dtype)
    return out
```

```python
from contextlib import ExitStack

import numpy as np

import concourse.bass as bass
from concourse import mybir
from concourse.bass import ds

F32 = mybir.dt.float32
F32R = mybir.dt.float32r
ALU = mybir.AluOpType
ACT = mybir.ActivationFunctionType

BATCH, C, H, W = 4, 128, 128, 128
ROWS = 4
T = ROWS * W
TILES = H // ROWS
HALVES = 2
DS = 16
TAPS = 9
MODES = 16
RING = 2
BC_BANKS = 3
PADW = W + 2
LN_EXP = "natural_log_exp_and_others"
EXP_TANH = "exp_and_others"


def shape_tables():
    f = np.float64
    eye = np.eye(C, dtype=f)
    mean = np.full((C, C), 1.0 / C)
    group = np.kron(np.eye(C // 4), np.full((4, 4), 0.25))
    state_sel = np.zeros((C, 2 * DS))
    for n in range(2 * DS):
        state_sel[32 + n, n] = state_sel[64 + n, n] = 1.0
    tap_sel = np.zeros((C, TAPS, C))
    for k in range(TAPS):
        for m in range(C):
            tap_sel[m // 32 * TAPS + k, k, m] = tap_sel[64 + m // 32 * TAPS + k, k, m] = 1.0
    two_pi = 2 * np.pi / W
    w, fr, hh = np.arange(W), np.arange(MODES), np.arange(H)
    fw = np.zeros((W, MODES, 2))
    fw[:, :, 0], fw[:, :, 1] = np.cos(two_pi * np.outer(w, fr)), -np.sin(two_pi * np.outer(w, fr))
    cos_h, sin_h = np.cos(two_pi * np.outer(hh, fr)), np.sin(two_pi * np.outer(hh, fr))
    fh = np.stack([np.stack([cos_h, -sin_h], 1), np.stack([sin_h, cos_h], 1)], 1)
    rot = np.zeros((2, 2, MODES, 2, MODES))
    for axis, phase in ((0, fr[None, :] + 0 * fr[:, None]), (1, fr[:, None] + 0 * fr[None, :])):
        for r in range(2):
            rot[axis, 0, :, r, :] = np.cos(two_pi * phase)
            rot[axis, 1, :, r, :] = (1, -1)[r] * np.sin(two_pi * phase)
    ta = np.zeros((4, 2, MODES, TILES, ROWS, 4, 2))
    for fy in range(4):
        c, s = (np.transpose(v.reshape(TILES, ROWS, MODES), (2, 0, 1)) for v in (cos_h, sin_h))
        ta[fy, 0, :, :, :, fy, 0], ta[fy, 1, :, :, :, fy, 0] = c, -s
        ta[fy, 0, :, :, :, fy, 1], ta[fy, 1, :, :, :, fy, 1] = s, c
    tb = np.zeros((4, ROWS, 4, 2, ROWS, W))
    for j in range(4):
        for r in range(ROWS):
            for fy in range(4):
                ph = two_pi * (4 * j + fy) * w
                tb[j, r, fy, 0, r], tb[j, r, fy, 1, r] = np.cos(ph) / (H * W), -np.sin(ph) / (H * W)
    return {
        "t_square": np.stack([eye, eye - mean, mean, group], 1).reshape(C, 4 * C),
        "t_state_sel": state_sel, "t_tap_sel": tap_sel.reshape(C, TAPS * C),
        "t_fw": fw.reshape(W, 32), "t_fh": fh.reshape(H, 64), "t_rot": rot.reshape(1, -1),
        "t_ta": ta.reshape(C, TILES * 32), "t_tb": tb.reshape(C, T),
    }


def build(nc, io, out):
    ctx = ExitStack()
    with ctx:
        def sb(name, shape, dt=F32):
            return ctx.enter_context(nc.sbuf_tensor(name, shape, dt))

        def sem(name):
            return ctx.enter_context(nc.semaphore(name))

        xres = sb("xres", [C, (H + 2) * W])
        square = sb("square", [C, 4 * C])
        ident, center, meanmat, groupmat = (square[:, C * k:C * (k + 1)] for k in range(4))
        state_sel = sb("state_sel", [C, 2 * DS, C], F32R)
        tap_sel = sb("tap_sel", [C, TAPS, C], F32R)
        hl = [sb(f"hl{p}", [C, T], F32R) for p in range(2)]
        w_in = sb("w_in", [C, 4 * C])
        w_x = sb("w_x", [C, HALVES, C])
        w_dt = sb("w_dt", [C, HALVES, C])
        w_out = sb("w_out", [C, HALVES, C])
        w_kg = sb("w_kg", [C, TAPS, C])
        w_pw = sb("w_pw", [C, C])
        a_neg = sb("a_neg", [C, HALVES, DS])
        state = sb("state", [C, HALVES, DS])
        conv_w = sb("conv_w", [C, HALVES, 4])
        cols = sb("cols", [C, 40])
        (ln_w, ln_b, eps_gn, b_kg, b_pw, b_e, b_l3, b_one) = (cols[:, k:k + 1] for k in range(8))
        bias_in, conv_b, dt_b, d_skip = (cols[:, 8:12], cols[:, 12:14], cols[:, 14:16], cols[:, 16:18])
        conv_b3, gmean, grstd, dmean, gvar, se, se_b = (
            cols[:, 18:20], cols[:, 20:21], cols[:, 21:22], cols[:, 22:23], cols[:, 23:24],
            cols[:, 24:25], cols[:, 25:26])
        avg, se_mid, se_exp, glog, mv = (
            cols[:, 26:27], cols[:, 27:28], cols[:, 28:29], cols[:, 29:30], cols[:, 30:32])
        zero3, spare = cols[:, 32:38], cols[:, 38:39]
        ones = sb("ones", [C, HALVES])
        ones2 = ones[:, :].unsqueeze(2)
        stats = sb("stats", [C, TILES, 6])

        ARENA = 25100
        arena = sb("arena", [C, ARENA])
        at = [0]

        def take(n, k=None):
            a = arena[:, at[0]:at[0] + n]
            at[0] += n
            assert at[0] <= ARENA
            return a

        def halves(n=T):
            return take(HALVES * n).rearrange("p (h t) -> p h t", h=HALVES)

        xin = [halves(T + 3) for _ in range(2)]
        tmp_z, tmp_u = halves(), halves()
        g_tile, sq, rs, xn, dts = (take(T) for _ in range(5))
        u, zs, delta, du = ([halves() for _ in range(2)] for _ in range(4))
        yd = halves()
        dA, dBu, hst, prod = ([halves() for _ in range(RING)] for _ in range(4))
        b_sb = [take(T) for _ in range(RING)]

        at[0] = 0
        w2 = take(TAPS * C).rearrange("p (k o) -> p k o", k=TAPS)
        w3 = take(TAPS * C).rearrange("p (k o) -> p k o", k=TAPS)
        se_w1, se_w2 = take(C), take(C)
        tab_a = take(TILES * 32)
        tab_b = take(T)
        fw, fh, rot = take(32), take(64), take(4 * 512)
        win = [take(6 * PADW).rearrange("p (r w) -> p r w", r=6) for _ in range(2)]
        sum_pool, sum_dve = take(T), take(T)
        gated = [take(T) for _ in range(2)]
        over = take(4608)
        prods = over.rearrange("p (k t) -> p k t", k=TAPS)
        row_t = [over[:, T * k:T * (k + 1)] for k in range(2)]
        g_norm = [over[:, T * (k + 2):T * (k + 3)] for k in range(2)]
        over = take(4608)
        dft_w = over[:, 0:4096].rearrange("p (h f) -> p h f", h=H)
        x_tap = over.rearrange("p (k f) -> p k f", k=TAPS)
        dft_wt = take(4096).rearrange("p (f c) -> p f c", f=32)
        rot_tmp = gated[0]
        o_t = take(T).rearrange("p (j k) -> p j k", j=4)
        ta = [take(32) for _ in range(2)]
        low = [take(C) for _ in range(2)]
        out_buf = [sum_pool, sum_dve]

        bank = [ctx.enter_context(nc.psum_tensor(f"bank{k}", [C, T], F32)) for k in range(8)]
        work0, work1 = bank[0], bank[1]
        b_ps, c_ps, y_ps = bank[2:4], bank[4:6], bank[6:8]

        names = """weights_in tables_in late_in prep_pool prep_dve prep_pe prep_act
            stats_done mv_ready gmean_ps gmean_ready gvar_ready gvar_ps glog_ready grstd_ready gn_ready
            g_ready cen_ready sq_ready var_ready lnv_ready rs_ready xn_ready xin_ready xin_evac hist_done
            z_ready z_evac zs_ready tap_done thu_ready u_ready xdbl_ready dts_ready hh_ready l_ready
            dt_ready v_done abs_done exp_done sp_ready delta_ready du_ready
            bbc_ready bs_ready dbu_ready da_ready scan_ready st_saved cbc_ready prod_ready prod_used
            yd_ready yz_ready proj_ready x0_upd
            win1 kern_ready kh_ready kl_ready bc_ready prod1_ready addp_done sump_ready addd_done
            sumd_ready pw_ready x1_upd
            avg_ready se1_ps se1_ready se2_ps seexp_ready seadd_ready se_ready seb_ready
            win2 conv2_ready gated_ready x2_upd
            g3_ready rowt_ps rowt_ready dftw_ps dftw_ready dftt_ps dftt_ready spec_ps
            xt_ready rot1_done rot2_done o_ps o_ready ta_ready low_ps low_ready
            win3 conv3_ready out_ready pads_done""".split()
        S = {n: sem(n) for n in names}
        x_in = [sem(f"x_in{k}") for k in range(8)]
        stored = [sem(f"stored{p}") for p in range(2)]

        def px(i, rows=ROWS, up=0):
            return xres[:, ds(W * (1 - up) + T * i, rows * W)]

        def pairs(eng, tile):
            tile(0, 0, 0, False)
            tile(1, 1, 1, False)
            with eng.Fori(1, TILES // 2 - 1) as k:
                tile(2 * k, 0, 2, False)
                tile(2 * k + 1, 1, 2, False)
            tile(TILES - 2, 0, 2, False)
            tile(TILES - 1, 1, 2, True)

        loads = [
            (square[:, :], io["t_square"]), (w_in[:, :], io["w_in"]),
            (w_x[:, :, 0:8], io["w_x"][:, :, 0:8]), (w_x[:, :, 32:64], io["w_x"][:, :, 8:40]),
            (w_x[:, :, 64:96], io["w_x"][:, :, 8:40]), (w_dt[0:8, :, :], io["w_dt"]),
            (w_out[:, :, :], io["w_out"]), (a_neg[:, :, :], io["a_log"]),
            (conv_w[:, :, :], io["conv_w"]), (ln_w, io["ln_w"]), (ln_b, io["ln_b"]),
            (conv_b, io["conv_b"]), (dt_b, io["b_dt"]), (d_skip, io["d"]),
            (b_kg[0:36, :], io["b_kg"]), (b_kg[64:100, :], io["b_kg"]), (b_pw, io["b_pw"]),
            (b_e, io["b_e"]), (b_l3, io["b_l3"]), (b_one, io["b_one"].partition_broadcast(C)),
            (arena[:, 0:TAPS * C], io["t_tap_sel"]), (arena[:, 2048:2048 + 2 * DS], io["t_state_sel"]),
        ]
        for g in range(4):
            lo = 32 * g
            for first in (0, 64):
                loads.append((w_kg[lo:lo + 32, :, first + TAPS * g:first + TAPS * (g + 1)], io["w_kg"][g]))
            loads.append((w_pw[lo:lo + 32, lo:lo + 32], io["w_pw"][g]))
        loaded = 16 * len(loads)

        block = ctx.enter_context(nc.Block())

        @block.sync
        def _(sp):
            for name in ("bs_ready", "dbu_ready", "scan_ready", "st_saved", "prod_ready", "prod_used"):
                sp.sem_inc(S[name], RING)
            sp.sem_inc(S["prod1_ready"], BC_BANKS)
            for p in range(2):
                sp.sem_inc(stored[p], 16)
            sp.wait_ge(S["prep_pool"], 5)
            for dst, src in loads:
                sp.dma_start(dst, src).then_inc(S["weights_in"], 16)
            with sp.Fori(0, BATCH) as b:
                for p in range(2):
                    sp.wait_ge(stored[p], 16 * (TILES // 2) * b + 16)
                for k in range(8):
                    sp.dma_start(xres[:, W + 2048 * k:W + 2048 * (k + 1)],
                                 io["x"][ds(b, 1), :, 2048 * k:2048 * (k + 1)].rearrange("b c t -> (b c) t")
                                 ).then_inc(x_in[k], 16)
                sp.wait_ge(S["x0_upd"], TILES * (b + 1))
                for dst, src in ((w2, io["w2"]), (w3, io["w3"]), (se_w1, io["se_w1"]), (se_w2, io["se_w2"]),
                                 (tab_a, io["t_ta"]), (tab_b, io["t_tb"]), (fw, io["t_fw"]), (fh, io["t_fh"]),
                                 (rot, io["t_rot"].partition_broadcast(C))):
                    sp.dma_start(dst, src).then_inc(S["late_in"], 16)

                def store(i, p, seen, last):
                    sp.wait_ge(S["out_ready"], TILES * b + i + 1)
                    sp.dma_start(out[ds(b, 1), :, ds(T * i, T)].rearrange("b c t -> (b c) t"),
                                 out_buf[p]).then_inc(stored[p], 16)
                pairs(sp, store)
            for p in range(2):
                sp.wait_ge(stored[p], 16 * (TILES // 2) * BATCH + 16)

        @block.tensor
        def _(pe):
            def mm(dst, lhs, rhs, start=True, stop=True):
                return pe.matmul(dst, lhs, rhs, start=start, stop=stop)

            pe.wait_ge(S["weights_in"], loaded)
            for k in range(4):
                last_mm = mm(work0[:, k:k + 1], w_in[:, C * k:C * (k + 1)], ln_b)
            last_mm.then_inc(S["prep_pe"], 1)
            pe.wait_ge(S["prep_dve"], 4)

            with pe.Fori(0, BATCH) as b:
                def group_norm(layer):
                    s = 4 * b + layer + 1
                    pe.wait_ge(S["mv_ready"], s)
                    mm(work0[:, 0:1], groupmat, mv[:, 0:1]).then_inc(S["gmean_ps"], 1)
                    pe.wait_ge(S["gvar_ready"], s)
                    mm(work1[:, 0:1], groupmat, gvar).then_inc(S["gvar_ps"], 1)

                group_norm(0)

                def pre(t, r, step):
                    if step == 0:
                        pe.wait_ge(S["g_ready"], t + 1)
                        mm(work0[:, :], center, g_tile).then_inc(S["cen_ready"], 1)
                    if step == 2:
                        pe.wait_ge(S["sq_ready"], t + 1)
                        mm(work1[:, :], meanmat, sq).then_inc(S["var_ready"], 1)
                    if step == 5:
                        pe.wait_ge(S["xn_ready"], t + 1)
                        mm(work0[:, :], w_in[:, 0:C], xn).then_inc(S["xin_ready"], 1)
                        mm(work1[:, :], w_in[:, C:2 * C], xn).then_inc(S["xin_ready"], 1)
                    if step == 6:
                        pe.wait_ge(S["xin_evac"], 2 * t + 1)
                        mm(work0[:, :], w_in[:, 2 * C:3 * C], xn).then_inc(S["z_ready"], 1)
                        pe.wait_ge(S["xin_evac"], 2 * t + 2)
                        mm(work1[:, :], w_in[:, 3 * C:4 * C], xn).then_inc(S["z_ready"], 1)
                    if step == 9:
                        pe.wait_ge(S["z_evac"], 2 * t + 1)
                        pe.wait_ge(S["u_ready"], t + 1)
                        mm(work0[:, :], w_x[:, 0, :], u[r][:, 0, :], stop=False)
                        mm(work0[:, :], w_x[:, 1, :], u[r][:, 1, :], start=False).then_inc(S["xdbl_ready"], 1)
                    if step == 10:
                        pe.wait_ge(S["dts_ready"], t + 1)
                        mm(work1[:, :], w_dt[:, 0, :], dts).then_inc(S["dt_ready"], 1)
                        pe.wait_ge(S["hh_ready"], t + 1)
                        mm(work0[:, :], w_dt[:, 1, :], dts).then_inc(S["dt_ready"], 1)

                def post(t, r, after_var):
                    if after_var:
                        pe.wait_ge(S["lnv_ready"], t + 3)
                    pe.wait_ge(S["yz_ready"], t + 1)
                    mm(work1[:, :], w_out[:, 0, :], yd[:, 0, :], stop=False)
                    mm(work1[:, :], w_out[:, 1, :], yd[:, 1, :], start=False).then_inc(S["proj_ready"], 1)

                def bcast_b(t, r, n):
                    q = DS * t + n
                    if n == 0:
                        pe.wait_ge(S["l_ready"], t + 1)
                    pe.wait_ge(S["bs_ready"], q + 1)
                    mm(b_ps[n % 2][:, :], state_sel[:, n, :], hl[r][:, :]).then_inc(S["bbc_ready"], 1)

                def bcast_c(t, r, n):
                    q = DS * t + n
                    pe.wait_ge(S["prod_ready"], q + 1)
                    mm(c_ps[n % 2][:, :], state_sel[:, DS + n, :], hl[r][:, :]).then_inc(S["cbc_ready"], 1)

                def sum_y(t, n, wait_y):
                    q = DS * t + n
                    pe.wait_ge(S["prod_ready"], q + 1 + RING)
                    if wait_y:
                        pe.wait_ge(S["yd_ready"], t)
                    for h in range(HALVES):
                        m = mm(y_ps[h][:, :], ident, prod[n % 2][:, h, :], start=(n == 0), stop=(n == DS - 1))
                    m.then_inc(S["prod_used"], 1)

                t0 = TILES * b
                for step in (0, 2, 5, 6, 9, 10):
                    pre(t0, 0, step)
                for n in range(4):
                    bcast_b(t0, 0, n)
                bcast_c(t0, 0, 0)

                def tile0(i, p, seen, last):
                    t = TILES * b + i
                    for n in range(DS):
                        if n + 4 < DS:
                            bcast_b(t, p, n + 4)
                        elif not last:
                            bcast_b(t + 1, 1 - p, n + 4 - DS)
                        if n + 1 < DS:
                            bcast_c(t, p, n + 1)
                        elif not last:
                            bcast_c(t + 1, 1 - p, 0)
                        if seen and n == 0:
                            sum_y(t - 1, DS - 1, False)
                        if n >= 1:
                            sum_y(t, n - 1, n == 1 and seen)
                        if not last:
                            pre(t + 1, 1 - p, n)
                        if n == 4 and seen:
                            post(t - 1, 1 - p, not last)
                        if n == 4 and seen and not last:
                            pe.wait_ge(S["x0_upd"], t)
                pairs(pe, tile0)
                sum_y(t0 + TILES - 1, DS - 1, False)
                post(t0 + TILES - 1, 1, False)

                group_norm(1)

                def kern(t, p, k):
                    if k == 0:
                        pe.wait_ge(S["win1"], t + 1)
                    m = mm(bank[2 + p][:, :].rearrange("p (r w) -> p r w", r=ROWS), w_kg[:, k, :],
                           win[p][:, k // 3:k // 3 + ROWS, k % 3:k % 3 + W], start=(k == 0), stop=(k == TAPS - 1))
                    if k == TAPS - 1:
                        m.then_inc(S["kern_ready"], 1)

                def pointwise(t, p):
                    pe.wait_ge(S["sump_ready"], t + 1)
                    mm(bank[p][:, :], w_pw[:, :], sum_pool, stop=False)
                    pe.wait_ge(S["sumd_ready"], t + 1)
                    mm(bank[p][:, :], w_pw[:, :], sum_dve, start=False).then_inc(S["pw_ready"], 1)

                for k in range(TAPS):
                    kern(t0, 0, k)

                def tile1(i, p, seen, last):
                    t = TILES * b + i
                    for k in range(TAPS):
                        if k == 0:
                            pe.wait_ge(S["kl_ready"], t + 1)
                        pe.wait_ge(S["prod1_ready"], TAPS * t + k + 1)
                        mm(bank[4 + k % BC_BANKS][:, :], tap_sel[:, k, :], hl[p][:, :]).then_inc(S["bc_ready"], 1)
                        if not last:
                            kern(t + 1, 1 - p, k)
                        if k == 4 and seen:
                            pointwise(t - 1, 1 - p)
                pairs(pe, tile1)
                pointwise(t0 + TILES - 1, 1)

                group_norm(2)
                pe.wait_ge(S["late_in"], 16 * 9 * (b + 1))
                pe.wait_ge(S["avg_ready"], b + 1)
                mm(work0[:, 0:1], se_w1, avg).then_inc(S["se1_ps"], 1)
                pe.wait_ge(S["se1_ready"], b + 1)
                mm(work1[:, 0:1], se_w2, se_mid).then_inc(S["se2_ps"], 1)

                def conv(dst, w, p, k, stop):
                    return mm(dst[:, :].rearrange("p (r w) -> p r w", r=ROWS), w[:, k, :],
                              win[p][:, k // 3:k // 3 + ROWS, k % 3:k % 3 + W], start=(k == 0), stop=stop)

                def tile2(i, p, seen, last):
                    t = TILES * b + i
                    pe.wait_ge(S["win2"], t + 1)
                    if seen == 2:
                        pe.wait_ge(S["gated_ready"], t - 1)
                    for k in range(TAPS):
                        m = conv(bank[2 + p], w2, p, k, k == TAPS - 1)
                    m.then_inc(S["conv2_ready"], 1)
                pairs(pe, tile2)

                group_norm(3)

                def spectrum(i, p, seen, last):
                    t = TILES * b + i
                    pe.wait_ge(S["g3_ready"], t + 1)
                    if seen == 2:
                        pe.wait_ge(S["rowt_ready"], t - 1)
                    for r in range(ROWS):
                        m = pe.transpose(bank[2 + p][:, W * r:W * (r + 1)], g_norm[p][:, W * r:W * (r + 1)], ident)
                    m.then_inc(S["rowt_ps"], 1)
                    if seen:
                        dft_rows(t - 1, 1 - p)
                    if last:
                        dft_rows(t, p)

                def dft_rows(t, p):
                    pe.wait_ge(S["rowt_ready"], t + 1)
                    for r in range(ROWS):
                        m = mm(bank[4 + p][:, 32 * r:32 * (r + 1)], row_t[p][:, W * r:W * (r + 1)], fw)
                    m.then_inc(S["dftw_ps"], 1)
                pairs(pe, spectrum)
                pe.wait_ge(S["dftw_ready"], t0 + TILES)
                for j in range(8):
                    if j >= 2:
                        pe.wait_ge(S["dftt_ready"], 8 * b + j - 1)
                    for f in range(4):
                        m = pe.transpose(bank[2 + j % 2][:, C * f:C * (f + 1)], dft_w[:, :, 4 * j + f], ident)
                    m.then_inc(S["dftt_ps"], 1)
                pe.wait_ge(S["dftt_ready"], 8 * (b + 1))
                for fy in range(MODES):
                    mm(work0[:, 32 * fy:32 * (fy + 1)], dft_wt[:, 2 * fy, :], fh[:, 0:32], stop=False)
                    m = mm(work0[:, 32 * fy:32 * (fy + 1)], dft_wt[:, 2 * fy + 1, :], fh[:, 32:64], start=False)
                m.then_inc(S["spec_ps"], 1)
                for k in range(TAPS):
                    pe.wait_ge(S["xt_ready"], TAPS * b + k + 1)
                    for j in range(4):
                        m = mm(bank[2 + j][:, 0:C], x_tap[:, k, C * j:C * (j + 1)], w3[:, k, :],
                               start=(k == 0), stop=(k == TAPS - 1))
                m.then_inc(S["o_ps"], 1)

                def low_rows(t, p):
                    pe.wait_ge(S["ta_ready"], t + 1)
                    for j in range(4):
                        m = mm(bank[6 + p][32 * j:32 * (j + 1), 0:C], ta[p], o_t[:, j, :])
                    m.then_inc(S["low_ps"], 1)

                pe.wait_ge(S["o_ready"], b + 1)
                low_rows(t0, 0)

                def tile3(i, p, seen, last):
                    t = TILES * b + i
                    pe.wait_ge(S["win3"], t + 1)
                    if seen == 2:
                        pe.wait_ge(S["out_ready"], t - 1)
                    for k in range(TAPS):
                        conv(bank[4 + p], w3, p, k, False)
                    if not last:
                        low_rows(t + 1, 1 - p)
                    pe.wait_ge(S["low_ready"], t + 1)
                    mm(bank[4 + p][:, :], low[p], tab_b, start=False).then_inc(S["conv3_ready"], 1)
                pairs(pe, tile3)

        @block.scalar
        def _(act):
            act.preload_act_table_set(LN_EXP)
            act.wait_ge(S["weights_in"], loaded)
            act.activation(a_neg[:, :, :], a_neg[:, :, :], ACT.Exp).then_inc(S["prep_act"], 1)

            with act.Fori(0, BATCH) as b:
                def group_norm(layer):
                    s = 4 * b + layer + 1
                    act.wait_ge(S["gvar_ps"], s)
                    act.activation(glog, work1[:, 0:1], ACT.Ln, bias=eps_gn).then_inc(S["glog_ready"], 1)
                    act.wait_ge(S["glog_ready"], s)
                    act.activation(grstd, glog, ACT.Exp, scale=-0.5).then_inc(S["grstd_ready"], 1)

                act.preload_act_table_set(LN_EXP)
                group_norm(0)

                def pre(t, r, step, start=False):
                    if step == 1:
                        act.wait_ge(S["cen_ready"], t + 1)
                        act.activation(sq, work0[:, :], ACT.Square).then_inc(S["sq_ready"], 1)
                    if step == 2:
                        act.wait_ge(S["var_ready"], t + 1)
                        act.activation(rs, work1[:, :], ACT.Ln, bias=eps_gn).then_inc(S["lnv_ready"], 1)
                    if step == 3:
                        act.wait_ge(S["lnv_ready"], t + 1)
                        act.activation(rs, rs, ACT.Exp, scale=-0.5).then_inc(S["rs_ready"], 1)
                    if step in (5, 6):
                        h = step - 5
                        if h == 0:
                            if start:
                                prev = zero3.rearrange("p (h t) -> p h t", h=HALVES)
                            else:
                                act.wait_ge(S["xin_evac"], 2 * t)
                                prev = xin[1 - r][:, :, T:T + 3]
                            act.activation(xin[r][:, :, 0:3], prev, ACT.Copy).then_inc(S["hist_done"], 1)
                        act.wait_ge(S["xin_ready"], 2 * t + h + 1)
                        src = (work0, work1)[h]
                        act.activation(xin[r][:, h, 3:T + 3], src[:, :], ACT.Identity, bias=bias_in[:, h:h + 1])
                        act.activation(u[r][:, h, :], src[:, :], ACT.Identity, scale=conv_w[:, h, 3:4],
                                       bias=conv_b3[:, h:h + 1]).then_inc(S["xin_evac"], 1)
                    if step == 7:
                        for h in range(HALVES):
                            act.wait_ge(S["z_ready"], 2 * t + h + 1)
                            src = (work0, work1)[h]
                            act.activation(zs[r][:, h, :], src[:, :], ACT.Identity, bias=bias_in[:, 2 + h:3 + h])
                            act.activation(tmp_z[:, h, :], src[:, :], ACT.Tanh,
                                           bias=bias_in[:, 2 + h:3 + h]).then_inc(S["z_evac"], 1)
                    if step == 8:
                        act.wait_ge(S["tap_done"], 6 * (t + 1))
                        act.activation(tmp_u, u[r], ACT.Tanh).then_inc(S["thu_ready"], 1)
                    if step == 9:
                        act.wait_ge(S["xdbl_ready"], t + 1)
                        act.activation(dts, work0[:, :], ACT.Copy).then_inc(S["dts_ready"], 1)
                        act.activation(hl[r][:, :], work0[:, :], ACT.Copy).then_inc(S["hh_ready"], 1)
                    if step == 10:
                        for h in range(HALVES):
                            act.wait_ge(S["dt_ready"], 2 * t + h + 1)
                            act.activation(delta[r][:, h, :], (work1, work0)[h][:, :], ACT.Identity,
                                           bias=dt_b[:, h:h + 1]).then_inc(S["v_done"], 1)
                    if step == 11:
                        act.wait_ge(S["zs_ready"], t + 1)
                        act.wait_ge(S["v_done"], 2 * t + 2)
                        act.activation(tmp_z, delta[r], ACT.Abs).then_inc(S["abs_done"], 1)
                    if step == 12:
                        act.wait_ge(S["abs_done"], t + 1)
                        act.activation(tmp_z, tmp_z, ACT.Exp, scale=-1.0).then_inc(S["exp_done"], 1)
                        act.preload_act_table_set(LN_EXP)
                        act.wait_ge(S["exp_done"], t + 1)
                        act.activation(tmp_z, tmp_z, ACT.Ln, bias=1.0).then_inc(S["sp_ready"], 1)

                def copy_b(t, n):
                    q = DS * t + n
                    act.wait_ge(S["bbc_ready"], q + 1)
                    act.wait_ge(S["dbu_ready"], q + 1)
                    act.activation(b_sb[n % 2], b_ps[n % 2][:, :], ACT.Copy).then_inc(S["bs_ready"], 1)

                def decay(t, r, n):
                    q = DS * t + n
                    if n == 0:
                        act.wait_ge(S["delta_ready"], t + 1)
                    act.wait_ge(S["scan_ready"], q + 1)
                    for h in range(HALVES):
                        a = act.activation(dA[n % 2][:, h, :], delta[r][:, h, :], ACT.Exp,
                                           scale=a_neg[:, h, n:n + 1])
                    a.then_inc(S["da_ready"], 1)

                t0 = TILES * b
                act.wait_ge(S["prep_dve"], 4)
                for step in range(DS):
                    pre(t0, 0, step, start=True)
                for n in range(2):
                    copy_b(t0, n)
                    decay(t0, 0, n)
                copy_b(t0, 2)

                def tile0(i, p, seen, last):
                    t = TILES * b + i
                    for n in range(DS):
                        if n + 3 < DS:
                            copy_b(t, n + 3)
                        elif not last:
                            copy_b(t + 1, n + 3 - DS)
                        if n + 2 < DS:
                            decay(t, p, n + 2)
                        elif not last:
                            decay(t + 1, 1 - p, n + 2 - DS)
                        if not last:
                            pre(t + 1, 1 - p, n)
                pairs(act, tile0)

                group_norm(1)

                def head(t, p):
                    act.wait_ge(S["kern_ready"], t + 1)
                    act.activation(hl[p][:, :], bank[2 + p][:, :], ACT.Identity, bias=b_kg).then_inc(S["kh_ready"], 1)

                head(t0, 0)

                def tile1(i, p, seen, last):
                    if not last:
                        head(TILES * b + i + 1, 1 - p)
                pairs(act, tile1)

                group_norm(2)
                act.wait_ge(S["se1_ps"], b + 1)
                act.activation(se_mid, work0[:, 0:1], ACT.Relu).then_inc(S["se1_ready"], 1)
                act.wait_ge(S["se2_ps"], b + 1)
                act.activation(se_exp, work1[:, 0:1], ACT.Exp, scale=-1.0).then_inc(S["seexp_ready"], 1)
                act.wait_ge(S["seb_ready"], b + 1)

                def tile2(i, p, seen, last):
                    t = TILES * b + i
                    act.wait_ge(S["conv2_ready"], t + 1)
                    if seen == 2:
                        act.wait_ge(S["x2_upd"], t - 1)
                    act.activation(gated[p], bank[2 + p][:, :], ACT.Identity, scale=se,
                                   bias=se_b).then_inc(S["gated_ready"], 1)
                pairs(act, tile2)

                group_norm(3)

                def spectrum(i, p, seen, last):
                    t = TILES * b + i
                    act.wait_ge(S["rowt_ps"], t + 1)
                    if seen == 2:
                        act.wait_ge(S["dftw_ps"], t - 1)
                    act.activation(row_t[p], bank[2 + p][:, :], ACT.Copy).then_inc(S["rowt_ready"], 1)
                pairs(act, spectrum)
                for j in range(8):
                    act.wait_ge(S["dftt_ps"], 8 * b + j + 1)
                    act.activation(dft_wt[:, 4 * j:4 * (j + 1), :],
                                   bank[2 + j % 2][:, :].rearrange("p (f c) -> p f c", f=4),
                                   ACT.Copy).then_inc(S["dftt_ready"], 1)
                act.wait_ge(S["o_ps"], b + 1)
                for j in range(4):
                    a = act.activation(o_t[:, j, :], bank[2 + j][:, 0:C], ACT.Copy)
                a.then_inc(S["o_ready"], 1)

                def tile3(i, p, seen, last):
                    t = TILES * b + i
                    act.wait_ge(S["low_ps"], t + 1)
                    if seen == 2:
                        act.wait_ge(S["conv3_ready"], t - 1)
                    act.activation(low[p], bank[6 + p][:, 0:C], ACT.Copy).then_inc(S["low_ready"], 1)
                pairs(act, tile3)

        @block.gpsimd
        def _(pool):
            for m in (w_x[:, :, :], w_dt[:, :, :], w_kg[:, :, :], w_pw[:, :]):
                pool.memset(m, 0.0).then_inc(S["prep_pool"], 1)
            pool.memset(ones[:, :], 1.0)
            pool.memset(cols[:, :], 0.0).then_inc(S["prep_pool"], 1)

            with pool.Fori(0, BATCH) as b:
                def input_gain(t, r):
                    pool.wait_ge(S["delta_ready"], t + 1)
                    pool.tensor_tensor(du[r], delta[r], u[r], ALU.mult).then_inc(S["du_ready"], 1)

                def drive(t, r, n):
                    q = DS * t + n
                    if n == 0:
                        pool.wait_ge(S["du_ready"], t + 1)
                    pool.wait_ge(S["bs_ready"], q + 1 + RING)
                    pool.wait_ge(S["scan_ready"], q + 1)
                    pool.tensor_tensor(dBu[n % 2], du[r], b_sb[n % 2].unsqueeze(1).broadcast_to([C, HALVES, T]),
                                       ALU.mult).then_inc(S["dbu_ready"], 1)

                def save(t, n):
                    pool.wait_ge(S["scan_ready"], DS * t + n + 1 + RING)
                    pool.tensor_tensor(state[:, :, n:n + 1], hst[n % 2][:, :, T - 1:T], ones2,
                                       ALU.mult).then_inc(S["st_saved"], 1)

                t0 = TILES * b
                input_gain(t0, 0)
                drive(t0, 0, 0)
                drive(t0, 0, 1)

                def tile0(i, p, seen, last):
                    t = TILES * b + i
                    for n in range(DS):
                        if not last and n == 14:
                            input_gain(t + 1, 1 - p)
                        if n + 2 < DS:
                            drive(t, p, n + 2)
                        elif not last:
                            drive(t + 1, 1 - p, n + 2 - DS)
                        save(t, n)
                pairs(pool, tile0)

                def tile1(i, p, seen, last):
                    t = TILES * b + i
                    pool.wait_ge(S["prod1_ready"], TAPS * t + 4 + BC_BANKS)
                    pool.tensor_tensor(prods[:, 0:2, :], prods[:, 0:2, :], prods[:, 2:4, :],
                                       ALU.add).then_inc(S["addp_done"], 1)
                    pool.wait_ge(S["addp_done"], t + 1)
                    if seen:
                        pool.wait_ge(S["pw_ready"], t)
                    pool.tensor_tensor(sum_pool, prods[:, 0, :], prods[:, 1, :], ALU.add).then_inc(S["sump_ready"], 1)
                pairs(pool, tile1)

                pool.wait_ge(S["late_in"], 16 * 9 * (b + 1))
                pool.wait_ge(S["o_ready"], b + 1)

                def tile3(i, p, seen, last):
                    t = TILES * b + i
                    if seen == 2:
                        pool.wait_ge(S["low_ps"], t - 1)
                    pool.tensor_tensor(ta[p], tab_a[:, ds(32 * i, 32)], ones[:, 0:1].broadcast_to([C, 32]),
                                       ALU.mult).then_inc(S["ta_ready"], 1)
                pairs(pool, tile3)

        @block.vector
        def _(dve):
            done = S["prep_dve"]
            dve.wait_ge(S["weights_in"], loaded)
            dve.wait_ge(S["prep_pe"], 1)
            dve.tensor_copy(tap_sel[:, :, :], arena[:, 0:TAPS * C].rearrange("p (k m) -> p k m", k=TAPS))
            dve.tensor_copy(state_sel[:, :, :], arena[:, 2048:2048 + 2 * DS].unsqueeze(2).broadcast_to([C, 2 * DS, C]))
            dve.memset(eps_gn, 1e-5)
            dve.tensor_scalar(w_in[:, 0:2 * C], w_in[:, 0:2 * C], ln_w, None, ALU.mult)
            dve.tensor_scalar(w_in[:, 2 * C:4 * C], w_in[:, 2 * C:4 * C], ln_w, 0.5, ALU.mult, ALU.mult)
            dve.tensor_scalar(bias_in[:, 0:2], work0[:, 0:2], 1.0, None, ALU.mult)
            dve.tensor_scalar(bias_in[:, 2:4], work0[:, 2:4], 0.5, None, ALU.mult)
            dve.tensor_tensor(b_l3, b_l3, b_one, ALU.add)
            dve.tensor_scalar(conv_b, conv_b, 0.5, None, ALU.mult)
            dve.tensor_scalar(conv_w[:, :, :], conv_w[:, :, :], 0.5, None, ALU.mult).then_inc(done, 1)
            dve.wait_ge(done, 1)
            dve.tensor_tensor(conv_b3, conv_w[:, :, 3:4].squeeze(2), bias_in[:, 0:2], ALU.mult).then_inc(done, 1)
            dve.wait_ge(done, 2)
            dve.tensor_tensor(conv_b3, conv_b3, conv_b, ALU.add).then_inc(done, 1)
            dve.wait_ge(S["prep_act"], 1)
            dve.tensor_scalar(a_neg[:, :, :], a_neg[:, :, :], -1.0, None, ALU.mult).then_inc(done, 1)
            dve.wait_ge(done, 4)

            with dve.Fori(0, BATCH) as b:
                def tile_stats(i):
                    dve.bn_stats(stats[:, ds(i, 1), :].rearrange("p a s -> p (a s)"), px(i)).then_inc(S["stats_done"], 1)

                def group_norm(layer):
                    s = 4 * b + layer + 1
                    dve.wait_ge(S["stats_done"], TILES * s)
                    dve.memset(spare, 0.0)
                    dve.bn_aggr(mv, stats[:, :, :].rearrange("p t s -> p (t s)")).then_inc(S["mv_ready"], 1)
                    dve.wait_ge(S["mv_ready"], s)
                    dve.wait_ge(S["gmean_ps"], s)
                    dve.tensor_copy(gmean, work0[:, 0:1]).then_inc(S["gmean_ready"], 1)
                    dve.wait_ge(S["gmean_ready"], 2 * s - 1)
                    dve.tensor_tensor(dmean, mv[:, 0:1], gmean, ALU.subtract).then_inc(S["gmean_ready"], 1)
                    dve.wait_ge(S["gmean_ready"], 2 * s)
                    dve.scalar_tensor_tensor(out=gvar, in0=dmean, scalar=dmean, in1=mv[:, 1:2], op0=ALU.mult,
                                             op1=ALU.add).then_inc(S["gvar_ready"], 1)
                    dve.wait_ge(S["grstd_ready"], s)

                def normalise(dst, src):
                    return dve.tensor_scalar(dst, src, gmean, grstd, ALU.subtract, ALU.mult)

                def window(i, p, counter):
                    normalise(win[p][:, :, 1:W + 1],
                              px(i, 6, 1).rearrange("p (r w) -> p r w", r=6)).then_inc(S[counter], 1)

                def pad_rows(layer):
                    for r in (0, H + 1):
                        dve.tensor_scalar(xres[:, W * r:W * (r + 1)], ident, 0.0, gmean, ALU.mult,
                                          ALU.add).then_inc(S["pads_done"], 1)
                    dve.wait_ge(S["pads_done"], 6 * b + 2 * layer)

                for k in range(8):
                    dve.wait_ge(x_in[k], 16 * (b + 1))
                    for j in range(4):
                        tile_stats(4 * k + j)

                group_norm(0)

                def taps(t, r, k):
                    for h in range(HALVES):
                        if k < 2:
                            dve.wait_ge(S["tap_done"], 6 * t + 2 * (2 - k) - 1 + h)
                        dve.scalar_tensor_tensor(out=u[r][:, h, :], in0=xin[r][:, h, k:k + T],
                                                 scalar=conv_w[:, h, k:k + 1], in1=u[r][:, h, :],
                                                 op0=ALU.mult, op1=ALU.add).then_inc(S["tap_done"], 1)

                def pre(t, i, r, step):
                    if step == 0:
                        normalise(g_tile, px(i)).then_inc(S["g_ready"], 1)
                    if step == 3:
                        dve.wait_ge(S["rs_ready"], t + 1)
                        dve.tensor_tensor(xn, work0[:, :], rs, ALU.mult).then_inc(S["xn_ready"], 1)
                    if step == 6:
                        dve.wait_ge(S["xin_evac"], 2 * t + 2)
                        taps(t, r, 2)
                    if step == 7:
                        taps(t, r, 1)
                        taps(t, r, 0)
                    if step == 8:
                        dve.wait_ge(S["thu_ready"], t + 1)
                        dve.scalar_tensor_tensor(out=u[r], in0=tmp_u, scalar=1.0, in1=u[r], op0=ALU.add,
                                                 op1=ALU.mult).then_inc(S["u_ready"], 1)
                    if step == 9:
                        dve.wait_ge(S["z_evac"], 2 * t + 2)
                        dve.scalar_tensor_tensor(out=zs[r], in0=tmp_z, scalar=1.0, in1=zs[r], op0=ALU.add,
                                                 op1=ALU.mult).then_inc(S["zs_ready"], 1)
                    if step == 10:
                        dve.wait_ge(S["hh_ready"], t + 1)
                        dve.tensor_tensor(hl[r][64:96, :], dts[64:96, :], hl[r][64:96, :].bitcast(F32),
                                          ALU.subtract).then_inc(S["l_ready"], 1)
                    if step == 13:
                        dve.wait_ge(S["sp_ready"], t + 1)
                        dve.scalar_tensor_tensor(out=delta[r], in0=delta[r], scalar=0.0, in1=tmp_z, op0=ALU.max,
                                                 op1=ALU.add).then_inc(S["delta_ready"], 1)

                def post(t, i, r, step):
                    if step == 1:
                        dve.wait_ge(S["prod_used"], DS * (t + 1) + RING)
                        for h in range(HALVES):
                            a = dve.scalar_tensor_tensor(out=yd[:, h, :], in0=u[r][:, h, :],
                                                         scalar=d_skip[:, h:h + 1], in1=y_ps[h][:, :],
                                                         op0=ALU.mult, op1=ALU.add)
                        a.then_inc(S["yd_ready"], 1)
                    if step == 2:
                        dve.wait_ge(S["yd_ready"], t + 1)
                        dve.tensor_tensor(yd, yd, zs[r], ALU.mult).then_inc(S["yz_ready"], 1)
                    if step == 5:
                        dve.wait_ge(S["proj_ready"], t + 1)
                        dve.tensor_tensor(px(i), work1[:, :], px(i), ALU.add).then_inc(S["x0_upd"], 1)
                    if step == 6:
                        dve.wait_ge(S["x0_upd"], t + 1)
                        tile_stats(i)

                def scan(t, n, start):
                    q = DS * t + n
                    dve.wait_ge(S["da_ready"], q + 1)
                    dve.wait_ge(S["dbu_ready"], q + 1 + RING)
                    dve.wait_ge(S["st_saved"], q + 1)
                    dve.wait_ge(S["prod_ready"], q + 1)
                    for h in range(HALVES):
                        a = dve.tensor_tensor_scan(hst[n % 2][:, h, :], dA[n % 2][:, h, :], dBu[n % 2][:, h, :],
                                                   0.0 if start else state[:, h, n:n + 1], ALU.mult, ALU.add)
                    a.then_inc(S["scan_ready"], 1)

                def read_out(t, n):
                    q = DS * t + n
                    dve.wait_ge(S["scan_ready"], q + 1 + RING)
                    dve.wait_ge(S["cbc_ready"], q + 1)
                    dve.wait_ge(S["prod_used"], q + 1)
                    dve.tensor_tensor(prod[n % 2], hst[n % 2], c_ps[n % 2][:, :].unsqueeze(1).broadcast_to(
                        [C, HALVES, T]), ALU.mult).then_inc(S["prod_ready"], 1)

                t0 = TILES * b
                for step in range(DS):
                    pre(t0, 0, 0, step)
                scan(t0, 0, True)

                def tile0(i, p, seen, last):
                    t = TILES * b + i
                    for n in range(DS):
                        if n + 1 < DS:
                            scan(t, n + 1, not seen)
                        elif not last:
                            scan(t + 1, 0, False)
                        read_out(t, n)
                        if seen:
                            post(t - 1, i - 1, 1 - p, n)
                        if not last:
                            pre(t + 1, i + 1, 1 - p, n)
                pairs(dve, tile0)
                for step in range(DS):
                    post(t0 + TILES - 1, TILES - 1, 1, step)

                group_norm(1)
                pad_rows(1)
                for p in range(2):
                    dve.memset(win[p][:, :, 0:1], 0.0)
                    dve.memset(win[p][:, :, W + 1:W + 2], 0.0)

                def rest(t, p):
                    dve.wait_ge(S["kh_ready"], t + 1)
                    dve.scalar_tensor_tensor(out=hl[p][64:128, :], in0=bank[2 + p][64:128, :],
                                             scalar=b_kg[64:128, :], in1=hl[p][64:128, :].bitcast(F32),
                                             op0=ALU.add, op1=ALU.subtract).then_inc(S["kl_ready"], 1)

                def update1(t, i, p):
                    dve.wait_ge(S["pw_ready"], t + 1)
                    dve.scalar_tensor_tensor(out=px(i), in0=bank[p][:, :], scalar=b_pw, in1=px(i),
                                             op0=ALU.add, op1=ALU.add).then_inc(S["x1_upd"], 1)

                window(0, 0, "win1")
                rest(t0, 0)

                def tile1(i, p, seen, last):
                    t = TILES * b + i
                    if not last:
                        window(i + 1, 1 - p, "win1")
                    for k in range(TAPS):
                        q = TAPS * t + k
                        dve.wait_ge(S["bc_ready"], q + 1)
                        dve.tensor_tensor(prods[:, k, :].rearrange("p (r w) -> p r w", r=ROWS),
                                          bank[4 + k % BC_BANKS][:, :].rearrange("p (r w) -> p r w", r=ROWS),
                                          win[p][:, k // 3:k // 3 + ROWS, k % 3:k % 3 + W],
                                          ALU.mult).then_inc(S["prod1_ready"], 1)
                        if k == 6 and seen:
                            update1(t - 1, i - 1, 1 - p)
                    if seen:
                        dve.wait_ge(S["x1_upd"], t)
                        tile_stats(i - 1)
                    dve.wait_ge(S["prod1_ready"], TAPS * (t + 1) + BC_BANKS)
                    dve.tensor_tensor(prods[:, 4:6, :], prods[:, 4:6, :], prods[:, 6:8, :],
                                      ALU.add).then_inc(S["addd_done"], 1)
                    dve.wait_ge(S["addd_done"], 2 * t + 1)
                    dve.tensor_tensor(prods[:, 4, :], prods[:, 4, :], prods[:, 5, :], ALU.add).then_inc(S["addd_done"], 1)
                    dve.wait_ge(S["addd_done"], 2 * t + 2)
                    dve.tensor_tensor(sum_dve, prods[:, 4, :], prods[:, 8, :], ALU.add).then_inc(S["sumd_ready"], 1)
                    dve.wait_ge(S["sump_ready"], t + 1)
                    if not last:
                        rest(t + 1, 1 - p)
                pairs(dve, tile1)
                update1(t0 + TILES - 1, TILES - 1, 1)
                dve.wait_ge(S["x1_upd"], t0 + TILES)
                tile_stats(TILES - 1)

                group_norm(2)
                pad_rows(2)
                dve.tensor_tensor(avg, dmean, grstd, ALU.mult).then_inc(S["avg_ready"], 1)
                dve.wait_ge(S["seexp_ready"], b + 1)
                dve.tensor_scalar(se, se_exp, 1.0, None, ALU.add).then_inc(S["seadd_ready"], 1)
                dve.wait_ge(S["seadd_ready"], b + 1)
                dve.reciprocal(se, se).then_inc(S["se_ready"], 1)
                dve.wait_ge(S["se_ready"], b + 1)
                dve.tensor_tensor(se_b, b_e, se, ALU.mult).then_inc(S["seb_ready"], 1)

                def update2(t, i, p):
                    dve.wait_ge(S["gated_ready"], t + 1)
                    dve.tensor_tensor(px(i), gated[p], px(i), ALU.add).then_inc(S["x2_upd"], 1)
                    dve.wait_ge(S["x2_upd"], t + 1)
                    tile_stats(i)

                window(0, 0, "win2")

                def tile2(i, p, seen, last):
                    t = TILES * b + i
                    if not last:
                        if seen:
                            dve.wait_ge(S["conv2_ready"], t)
                        window(i + 1, 1 - p, "win2")
                    if seen:
                        dve.wait_ge(S["win2"], t + (1 if last else 2))
                        update2(t - 1, i - 1, 1 - p)
                pairs(dve, tile2)
                update2(t0 + TILES - 1, TILES - 1, 1)

                group_norm(3)
                pad_rows(3)

                def spectrum(i, p, seen, last):
                    t = TILES * b + i
                    if seen == 2:
                        dve.wait_ge(S["rowt_ps"], t - 1)
                    normalise(g_norm[p], px(i)).then_inc(S["g3_ready"], 1)
                    if seen:
                        keep_rows(t - 1, i - 1, 1 - p)
                    if last:
                        keep_rows(t, i, p)

                def keep_rows(t, i, p):
                    dve.wait_ge(S["dftw_ps"], t + 1)
                    dve.tensor_copy(dft_w[:, ds(ROWS * i, ROWS), :],
                                    bank[4 + p][:, 0:32 * ROWS].rearrange("p (h f) -> p h f", h=ROWS)
                                    ).then_inc(S["dftw_ready"], 1)
                pairs(dve, spectrum)

                def rotate(dst, src, axis, k):
                    cos, sin = (rot[:, T * (2 * axis + a):T * (2 * axis + a + 1)] for a in range(2))
                    x4, s4, r4 = (v.rearrange("p (y r x) -> p y r x", y=MODES, r=2) for v in (src, sin, rot_tmp))
                    q = (TAPS - 1) * b + k
                    for r in range(2):
                        a = dve.tensor_tensor(r4[:, :, r, :], x4[:, :, 1 - r, :], s4[:, :, r, :], ALU.mult)
                    dve.tensor_tensor(dst, src, cos, ALU.mult).then_inc(S["rot1_done"], 1)
                    dve.wait_ge(S["rot1_done"], q)
                    dve.tensor_tensor(dst, dst, rot_tmp, ALU.add).then_inc(S["xt_ready"], 1)

                dve.wait_ge(S["spec_ps"], b + 1)
                dve.tensor_copy(x_tap[:, 0, :], work0[:, :]).then_inc(S["xt_ready"], 1)
                for k in range(1, TAPS):
                    axis, of = (1, k - 1) if k % 3 else (0, k - 3)
                    dve.wait_ge(S["xt_ready"], TAPS * b + k)
                    rotate(x_tap[:, k, :], x_tap[:, of, :], axis, k)

                window(0, 0, "win3")

                def store_tile(t, i, p):
                    dve.wait_ge(S["conv3_ready"], t + 1)
                    dve.wait_ge(stored[p], 8 * (t - p) + 16)
                    dve.scalar_tensor_tensor(out=out_buf[p], in0=bank[4 + p][:, :], scalar=b_l3, in1=px(i),
                                             op0=ALU.add, op1=ALU.add).then_inc(S["out_ready"], 1)

                def tile3(i, p, seen, last):
                    t = TILES * b + i
                    if not last:
                        if seen:
                            dve.wait_ge(S["conv3_ready"], t)
                        window(i + 1, 1 - p, "win3")
                    if seen:
                        store_tile(t - 1, i - 1, 1 - p)
                pairs(dve, tile3)
                store_tile(t0 + TILES - 1, TILES - 1, 1)


_SHAPE = (BATCH, C, H, W)


def kernel(**inputs):
    from concourse import bacc
    from concourse.bass_utils import run_bass_kernel_spmd

    x = {k: np.asarray(v) for k, v in inputs.items()}

    def halves(a):
        return a.reshape(HALVES, C, -1).transpose(1, 0, 2)

    def column(a):
        return a.reshape(-1, 1)

    def taps(a):
        return a.reshape(a.shape[0], a.shape[1], TAPS).transpose(1, 2, 0)

    arrays = {
        "x": x["x"].reshape(BATCH, C, H * W),
        "w_in": x["L0_conv_W_in"].T, "w_x": halves(x["L0_conv_W_xproj"].T),
        "w_dt": x["L0_conv_W_dt"].T.reshape(8, HALVES, C), "w_out": halves(x["L0_conv_W_out"].T),
        "a_log": halves(x["L0_conv_A_log"]), "conv_w": halves(x["L0_conv_conv_w"]),
        "ln_w": column(x["L0_conv_ln_w"]), "ln_b": column(x["L0_conv_ln_b"]),
        "conv_b": x["L0_conv_conv_b"].reshape(HALVES, C).T, "b_dt": x["L0_conv_b_dt"].reshape(HALVES, C).T,
        "d": x["L0_conv_D"].reshape(HALVES, C).T,
        "w_kg": x["L1_conv_w_kg"].reshape(4, TAPS, 32, TAPS).transpose(0, 2, 3, 1),
        "b_kg": column(x["L1_conv_b_kg"]), "w_pw": x["L1_conv_w_pw"].reshape(4, 32, 32).transpose(0, 2, 1),
        "b_pw": column(x["L1_conv_b_pw"]),
        "w2": taps(x["L2_conv_weight"][0]), "b_e": column(x["L2_conv_bias_e"][0]),
        "se_w1": np.pad(x["L2_conv_se_w1"].T, ((0, 0), (0, C - 16))),
        "se_w2": np.pad(x["L2_conv_se_w2"].T, ((0, C - 16), (0, 0))),
        "w3": taps(x["L3_conv_weight"]), "b_l3": column(x["L3_conv_conv_bias"]),
        "b_one": x["L3_conv_bias"].reshape(1, 1),
        **{k: v.astype(np.float32) for k, v in shape_tables().items()},
    }
    arrays = {f"in_{k}": np.ascontiguousarray(v) for k, v in arrays.items()}
    nc = bacc.Bacc("TRN2", target_bir_lowering=False, num_devices=1)
    io = {k[3:]: nc.dram_tensor(k, v.shape, F32, kind="ExternalInput").ap() for k, v in arrays.items()}
    out = nc.dram_tensor("out", (BATCH, C, H * W), F32, kind="ExternalOutput").ap()
    build(nc, io, out)
    done = run_bass_kernel_spmd(nc, [arrays], core_ids=[0])
    return done.results[0]["out"].reshape(_SHAPE)
```

```python
from contextlib import ExitStack

import numpy as np

import concourse.bass as bass
from concourse import mybir
from concourse.bass import ds

F32 = mybir.dt.float32
F32R = mybir.dt.float32r
ALU = mybir.AluOpType
ACT = mybir.ActivationFunctionType

BATCH, C, H, W = 4, 128, 128, 128
ROWS = 4
T = ROWS * W
TILES = H // ROWS
HALVES = 2
DS = 16
TAPS = 9
KERNELS = 4 * TAPS
MODES = 16
RING = 2
DEEP = 4
LEAD = 3
BC_BANKS = 3
PADW = W + 2
LN_EXP = "natural_log_exp_and_others"
EXP_TANH = "exp_and_others"


def shape_tables():
    f = np.float64
    eye = np.eye(C, dtype=f)
    mean = np.full((C, C), 1.0 / C)
    group = np.kron(np.eye(C // 4), np.full((4, 4), 0.25))
    state_sel = np.zeros((C, 2 * DS))
    for n in range(2 * DS):
        state_sel[32 + n, n] = state_sel[64 + n, n] = 1.0
    tap_sel = np.zeros((C, TAPS, C))
    for k in range(TAPS):
        for m in range(C):
            tap_sel[m // 32 * TAPS + k, k, m] = tap_sel[64 + m // 32 * TAPS + k, k, m] = 1.0
    shift_sel = np.zeros((C, 3, C))
    for kx in range(3):
        for m in range(KERNELS):
            shift_sel[KERNELS * kx + m, kx, m] = shift_sel[KERNELS * kx + m, kx, 64 + m] = 1.0
    two_pi = 2 * np.pi / W
    w, fr, hh = np.arange(W), np.arange(MODES), np.arange(H)
    fw = np.zeros((W, MODES, 2))
    fw[:, :, 0], fw[:, :, 1] = np.cos(two_pi * np.outer(w, fr)), -np.sin(two_pi * np.outer(w, fr))
    cos_h, sin_h = np.cos(two_pi * np.outer(hh, fr)), np.sin(two_pi * np.outer(hh, fr))
    fh = np.stack([np.stack([cos_h, -sin_h], 1), np.stack([sin_h, cos_h], 1)], 1)
    rot = np.zeros((2, 2, MODES, 2, MODES))
    for axis, phase in ((0, fr[None, :] + 0 * fr[:, None]), (1, fr[:, None] + 0 * fr[None, :])):
        for r in range(2):
            rot[axis, 0, :, r, :] = np.cos(two_pi * phase)
            rot[axis, 1, :, r, :] = (1, -1)[r] * np.sin(two_pi * phase)
    ta = np.zeros((4, 2, MODES, TILES, ROWS, 4, 2))
    for fy in range(4):
        c, s = (np.transpose(v.reshape(TILES, ROWS, MODES), (2, 0, 1)) for v in (cos_h, sin_h))
        ta[fy, 0, :, :, :, fy, 0], ta[fy, 1, :, :, :, fy, 0] = c, -s
        ta[fy, 0, :, :, :, fy, 1], ta[fy, 1, :, :, :, fy, 1] = s, c
    tb = np.zeros((4, ROWS, 4, 2, ROWS, W))
    for j in range(4):
        for r in range(ROWS):
            for fy in range(4):
                ph = two_pi * (4 * j + fy) * w
                tb[j, r, fy, 0, r], tb[j, r, fy, 1, r] = np.cos(ph) / (H * W), -np.sin(ph) / (H * W)
    return {
        "t_square": np.stack([eye, eye - mean, mean, group], 1).reshape(C, 4 * C),
        "t_state_sel": state_sel, "t_tap_sel": tap_sel.reshape(C, TAPS * C),
        "t_shift_sel": shift_sel.reshape(C, 3 * C),
        "t_fw": fw.reshape(W, 32), "t_fh": fh.reshape(H, 64), "t_rot": rot.reshape(1, -1),
        "t_ta": ta.reshape(C, TILES * 32), "t_tb": tb.reshape(C, T),
    }


def build(nc, io, out):
    ctx = ExitStack()
    with ctx:
        def sb(name, shape, dt=F32):
            return ctx.enter_context(nc.sbuf_tensor(name, shape, dt))

        def sem(name):
            return ctx.enter_context(nc.semaphore(name))

        xres = sb("xres", [C, (H + 2) * W])
        square = sb("square", [C, 4 * C])
        ident, center, meanmat, groupmat = (square[:, C * k:C * (k + 1)] for k in range(4))
        state_sel = sb("state_sel", [C, 2 * DS], F32R)
        tap_sel = sb("tap_sel", [C, TAPS, C], F32R)
        hl = [sb(f"hl{p}", [C, T], F32R) for p in range(2)]
        w_in = sb("w_in", [C, 4 * C])
        w_x = sb("w_x", [C, HALVES, C])
        w_dt = sb("w_dt", [C, HALVES, C])
        w_out = sb("w_out", [C, HALVES, C])
        w_kg = sb("w_kg", [C, 3, C])
        shift_sel = sb("shift_sel", [C, 3, C])
        w_pw = sb("w_pw", [C, C])
        a_neg = sb("a_neg", [C, HALVES, DS])
        state = sb("state", [C, HALVES, DS])
        conv_w = sb("conv_w", [C, HALVES, 4])
        cols = sb("cols", [C, 40])
        (ln_w, ln_b, eps_gn, b_kg, b_pw, b_e, b_l3, b_one) = (cols[:, k:k + 1] for k in range(8))
        bias_in, conv_b, dt_b, d_skip = (cols[:, 8:12], cols[:, 12:14], cols[:, 14:16], cols[:, 16:18])
        conv_b3, gmean, grstd, dmean, gvar, se, se_b = (
            cols[:, 18:20], cols[:, 20:21], cols[:, 21:22], cols[:, 22:23], cols[:, 23:24],
            cols[:, 24:25], cols[:, 25:26])
        avg, se_mid, se_exp, glog, mv = (
            cols[:, 26:27], cols[:, 27:28], cols[:, 28:29], cols[:, 29:30], cols[:, 30:32])
        zero3, spare = cols[:, 32:38], cols[:, 38:39]
        ones = sb("ones", [C, HALVES])
        ones2 = ones[:, :].unsqueeze(2)
        stats = sb("stats", [C, TILES, 6])

        ARENA = 27660
        arena = sb("arena", [C, ARENA])
        at = [0]

        def take(n, k=None):
            a = arena[:, at[0]:at[0] + n]
            at[0] += n
            assert at[0] <= ARENA
            return a

        def halves(n=T):
            return take(HALVES * n).rearrange("p (h t) -> p h t", h=HALVES)

        xin, tmp_z, tmp_u, du, yd = halves(T + 3), halves(), halves(), halves(), halves()
        g_tile, sq, rs = tmp_u[:, 0, :], tmp_u[:, 1, :], tmp_u[:, 0, :]
        xn, dts = take(T), take(T)
        u, zs, delta = ([halves() for _ in range(2)] for _ in range(3))
        hst = [halves() for _ in range(RING)]
        dA, dBu, prod = ([halves() for _ in range(DEEP)] for _ in range(3))
        b_sb = [take(T) for _ in range(RING)]

        at[0] = 0
        w2 = take(TAPS * C).rearrange("p (k o) -> p k o", k=TAPS)
        w3 = take(TAPS * C).rearrange("p (k o) -> p k o", k=TAPS)
        se_w1, se_w2 = take(C), take(C)
        tab_a = take(TILES * 32)
        tab_b = take(T)
        fw, fh, rot = take(32), take(64), take(4 * 512)
        win = [take(6 * PADW).rearrange("p (r w) -> p r w", r=6) for _ in range(2)]
        sum_pool, sum_dve = take(T), take(T)
        gated = [take(T) for _ in range(2)]
        by_column = take(ROWS * PADW).rearrange("p (r w) -> p r w", r=ROWS)
        over = take(4608)
        prods = [over.rearrange("p (k t) -> p k t", k=TAPS)]
        row_t = [over[:, T * k:T * (k + 1)] for k in range(2)]
        g_norm = [over[:, T * (k + 2):T * (k + 3)] for k in range(2)]
        over = take(4608)
        dft_w = over[:, 0:4096].rearrange("p (h f) -> p h f", h=H)
        x_tap = over.rearrange("p (k f) -> p k f", k=TAPS)
        prods.append(over.rearrange("p (k t) -> p k t", k=TAPS))
        dft_wt = take(4096).rearrange("p (f c) -> p f c", f=32)
        rot_tmp = gated[0]
        o_t = take(T).rearrange("p (j k) -> p j k", j=4)
        ta = [take(32) for _ in range(2)]
        low = [take(C) for _ in range(2)]
        out_buf = [sum_pool, sum_dve]

        bank = [ctx.enter_context(nc.psum_tensor(f"bank{k}", [C, T], F32)) for k in range(8)]
        work0, work1 = bank[0], bank[1]
        b_ps, c_ps, y_ps = bank[2:4], bank[4:6], bank[6:8]
        o_ps = bank[1:4] + bank[6:7]

        names = """weights_in tables_in late_in prep_pool prep_dve prep_pe prep_act
            stats_done mv_ready gmean_ps gmean_ready gvar_ready gvar_ps glog_ready grstd_ready gn_ready
            g_ready cen_ready sq_ready var_ready lnv_ready rs_ready xn_ready xin_ready xin_evac hist_done
            z_ready z_evac zs_ready tap_done thu_ready u_ready xdbl_ready dts_ready hh_ready l_ready
            dt_ready v_done abs_done exp_done sp_ready delta_ready du_ready
            bbc_ready bs_ready dbu_ready da_ready scan_ready st_saved cbc_ready prod_ready prod_used
            yd_ready yz_ready proj_ready x0_upd
            win1 bycol_ps bycol_ready kern_ready kh_ready kl_ready bc_ready prod1_ready addp_done
            sump_ready pw_ready x1_upd
            avg_ready se1_ps se1_ready se2_ps seexp_ready seadd_ready se_ready seb_ready
            win2 conv2_ready gated_ready x2_upd
            g3_ready rowt_ps rowt_ready dftw_ps dftw_ready dftt_ps dftt_ready spec_ps
            xt_ready rot1_done rot2_done o_ps o_ready ta_ready low_ps low_ready
            win3 conv3_ready out_ready pads_done""".split()
        S = {n: sem(n) for n in names}
        x_in = [sem(f"x_in{k}") for k in range(8)]
        stored = [sem(f"stored{p}") for p in range(2)]

        def px(i, rows=ROWS, up=0):
            return xres[:, ds(W * (1 - up) + T * i, rows * W)]

        def pairs(eng, tile):
            tile(0, 0, 0, 2)
            tile(1, 1, 1, 2)
            with eng.Fori(1, TILES // 2 - 1) as k:
                tile(2 * k, 0, 2, 2)
                tile(2 * k + 1, 1, 2, 2)
            tile(TILES - 2, 0, 2, 1)
            tile(TILES - 1, 1, 2, 0)

        loads = [
            (square[:, :], io["t_square"]), (shift_sel[:, :, :].rearrange("p k m -> p (k m)"), io["t_shift_sel"]), (w_in[:, :], io["w_in"]),
            (w_x[:, :, 0:8], io["w_x"][:, :, 0:8]), (w_x[:, :, 32:64], io["w_x"][:, :, 8:40]),
            (w_x[:, :, 64:96], io["w_x"][:, :, 8:40]), (w_dt[0:8, :, :], io["w_dt"]),
            (w_out[:, :, :], io["w_out"]), (a_neg[:, :, :], io["a_log"]),
            (conv_w[:, :, :], io["conv_w"]), (ln_w, io["ln_w"]), (ln_b, io["ln_b"]),
            (conv_b, io["conv_b"]), (dt_b, io["b_dt"]), (d_skip, io["d"]),
            (b_kg[0:36, :], io["b_kg"]), (b_kg[64:100, :], io["b_kg"]), (b_pw, io["b_pw"]),
            (b_e, io["b_e"]), (b_l3, io["b_l3"]), (b_one, io["b_one"].partition_broadcast(C)),
            (arena[:, 0:TAPS * C], io["t_tap_sel"]), (arena[:, 2048:2048 + 2 * DS], io["t_state_sel"]),
        ]
        for g in range(4):
            lo = 32 * g
            for kx in range(3):
                at_kx = KERNELS * kx + TAPS * g
                loads.append((w_kg[lo:lo + 32, :, at_kx:at_kx + TAPS], io["w_kg"][g, kx]))
            loads.append((w_pw[lo:lo + 32, lo:lo + 32], io["w_pw"][g]))
        loaded = 16 * len(loads)

        block = ctx.enter_context(nc.Block())

        @block.sync
        def _(sp):
            for name in ("bs_ready", "st_saved", "prod_ready", "dbu_ready", "dftw_ready",
                         "x1_upd"):
                sp.sem_inc(S[name], RING)
            for name in ("scan_ready", "prod_used"):
                sp.sem_inc(S[name], DEEP)
            sp.sem_inc(S["prod1_ready"], BC_BANKS)
            for p in range(2):
                sp.sem_inc(stored[p], 16)
            sp.wait_ge(S["prep_pool"], 5)
            for dst, src in loads:
                sp.dma_start(dst, src).then_inc(S["weights_in"], 16)
            with sp.Fori(0, BATCH) as b:
                for p in range(2):
                    sp.wait_ge(stored[p], 16 * (TILES // 2) * b + 16)
                for k in range(8):
                    sp.dma_start(xres[:, W + 2048 * k:W + 2048 * (k + 1)],
                                 io["x"][ds(b, 1), :, 2048 * k:2048 * (k + 1)].rearrange("b c t -> (b c) t")
                                 ).then_inc(x_in[k], 16)
                sp.wait_ge(S["x0_upd"], TILES * (b + 1))
                for dst, src in ((w2, io["w2"]), (w3, io["w3"]), (se_w1, io["se_w1"]), (se_w2, io["se_w2"]),
                                 (tab_a, io["t_ta"]), (tab_b, io["t_tb"]), (fw, io["t_fw"]), (fh, io["t_fh"]),
                                 (rot, io["t_rot"].partition_broadcast(C))):
                    sp.dma_start(dst, src).then_inc(S["late_in"], 16)

                def store(i, p, seen, left):
                    sp.wait_ge(S["out_ready"], TILES * b + i + 1)
                    sp.dma_start(out[ds(b, 1), :, ds(T * i, T)].rearrange("b c t -> (b c) t"),
                                 out_buf[p]).then_inc(stored[p], 16)
                pairs(sp, store)
            for p in range(2):
                sp.wait_ge(stored[p], 16 * (TILES // 2) * BATCH + 16)

        @block.tensor
        def _(pe):
            def mm(dst, lhs, rhs, start=True, stop=True):
                return pe.matmul(dst, lhs, rhs, start=start, stop=stop)

            pe.wait_ge(S["weights_in"], loaded)
            for k in range(4):
                last_mm = mm(work0[:, k:k + 1], w_in[:, C * k:C * (k + 1)], ln_b)
            last_mm.then_inc(S["prep_pe"], 1)
            pe.wait_ge(S["prep_dve"], 4)

            with pe.Fori(0, BATCH) as b:
                def group_norm(layer):
                    s = 4 * b + layer + 1
                    pe.wait_ge(S["mv_ready"], s)
                    mm(work0[:, 0:1], groupmat, mv[:, 0:1]).then_inc(S["gmean_ps"], 1)
                    pe.wait_ge(S["gvar_ready"], s)
                    mm(work1[:, 0:1], groupmat, gvar).then_inc(S["gvar_ps"], 1)

                group_norm(0)

                def front(t, step, first=False):
                    if step == 11:
                        pe.wait_ge(S["g_ready"], t + 1)
                        if not first:
                            pe.wait_ge(S["v_done"], 2 * t)
                        mm(work1[:, :], center, g_tile).then_inc(S["cen_ready"], 1)
                    if step == 13:
                        pe.wait_ge(S["sq_ready"], t + 1)
                        mm(work0[:, :], meanmat, sq).then_inc(S["var_ready"], 1)

                def back(t, r, step, seen=0):
                    if step == 0:
                        pe.wait_ge(S["xn_ready"], t + 1)
                        mm(work0[:, :], w_in[:, 0:C], xn).then_inc(S["xin_ready"], 1)
                        mm(work1[:, :], w_in[:, C:2 * C], xn).then_inc(S["xin_ready"], 1)
                    if step == 2:
                        pe.wait_ge(S["xin_evac"], 2 * t + 1)
                        mm(work0[:, :], w_in[:, 2 * C:3 * C], xn).then_inc(S["z_ready"], 1)
                    if step == 3:
                        pe.wait_ge(S["xin_evac"], 2 * t + 2)
                        mm(work1[:, :], w_in[:, 3 * C:4 * C], xn).then_inc(S["z_ready"], 1)
                    if step == 7:
                        pe.wait_ge(S["z_evac"], 2 * t + 1)
                        if seen:
                            pe.wait_ge(S["x0_upd"], t - 1)
                        pe.wait_ge(S["u_ready"], t + 1)
                        mm(work0[:, :], w_x[:, 0, :], u[r][:, 0, :], stop=False)
                        mm(work0[:, :], w_x[:, 1, :], u[r][:, 1, :], start=False).then_inc(S["xdbl_ready"], 1)
                    if step == 9:
                        pe.wait_ge(S["z_evac"], 2 * t + 2)
                        pe.wait_ge(S["dts_ready"], t + 1)
                        mm(work1[:, :], w_dt[:, 0, :], dts).then_inc(S["dt_ready"], 1)
                        pe.wait_ge(S["hh_ready"], t + 1)
                        mm(work0[:, :], w_dt[:, 1, :], dts).then_inc(S["dt_ready"], 1)

                def post(t, left):
                    if left:
                        pe.wait_ge(S["z_evac"], 2 * t + 5)
                    pe.wait_ge(S["yz_ready"], t + 1)
                    mm(work0[:, :], w_out[:, 0, :], yd[:, 0, :], stop=False)
                    mm(work0[:, :], w_out[:, 1, :], yd[:, 1, :], start=False).then_inc(S["proj_ready"], 1)

                def bcast_b(t, r, n):
                    q = DS * t + n
                    if n == 0:
                        pe.wait_ge(S["l_ready"], t + 1)
                    pe.wait_ge(S["bs_ready"], q + 1)
                    mm(b_ps[n % 2][:, :], state_sel[:, n:n + 1].broadcast_to([C, C]), hl[r][:, :]).then_inc(S["bbc_ready"], 1)

                def bcast_c(t, r, n):
                    q = DS * t + n
                    pe.wait_ge(S["prod_ready"], q + 1)
                    mm(c_ps[n % 2][:, :], state_sel[:, DS + n:DS + n + 1].broadcast_to([C, C]), hl[r][:, :]).then_inc(S["cbc_ready"], 1)

                def sum_y(t, n, wait_y):
                    q = DS * t + n
                    pe.wait_ge(S["prod_ready"], q + 1 + RING)
                    if wait_y:
                        pe.wait_ge(S["yd_ready"], t)
                    for h in range(HALVES):
                        m = mm(y_ps[h][:, :], ident, prod[n % DEEP][:, h, :], start=(n == 0), stop=(n == DS - 1))
                    m.then_inc(S["prod_used"], 1)

                t0 = TILES * b
                for step in range(DS):
                    front(t0, step, first=True)
                for step in range(DS):
                    back(t0, 0, step)
                    front(t0 + 1, step)
                for n in range(LEAD + 2):
                    bcast_b(t0, 0, n)
                bcast_c(t0, 0, 0)

                def tile0(i, p, seen, left):
                    t = TILES * b + i
                    for n in range(DS):
                        ahead = n + LEAD + 2
                        if ahead < DS:
                            bcast_b(t, p, ahead)
                        elif left:
                            bcast_b(t + 1, 1 - p, ahead - DS)
                        if n + 1 < DS:
                            bcast_c(t, p, n + 1)
                        elif left:
                            bcast_c(t + 1, 1 - p, 0)
                        if seen and n == 0:
                            sum_y(t - 1, DS - 1, False)
                        if n >= 1:
                            sum_y(t, n - 1, n == 1 and seen)
                        if left:
                            back(t + 1, 1 - p, n, seen)
                        if n == 5 and seen:
                            post(t - 1, left)
                        if left == 2:
                            front(t + 2, n)
                pairs(pe, tile0)
                sum_y(t0 + TILES - 1, DS - 1, False)
                pe.wait_ge(S["x0_upd"], t0 + TILES - 1)
                post(t0 + TILES - 1, 0)

                group_norm(1)

                def by_columns(t, p, ky):
                    if ky == 0:
                        pe.wait_ge(S["win1"], t + 1)
                    m = mm(bank[2][:, :].rearrange("p (r w) -> p r w", r=ROWS), w_kg[:, ky, :],
                           win[p][:, ky:ky + ROWS, 1:W + 1], start=(ky == 0), stop=(ky == 2))
                    if ky == 2:
                        m.then_inc(S["bycol_ps"], 1)

                def join_columns(t, kx):
                    if kx == 0:
                        pe.wait_ge(S["bycol_ready"], t + 1)
                    m = mm(bank[3][:, :].rearrange("p (r w) -> p r w", r=ROWS), shift_sel[:, kx, :],
                           by_column[:, :, kx:kx + W], start=(kx == 0), stop=(kx == 2))
                    if kx == 2:
                        m.then_inc(S["kern_ready"], 1)

                def pointwise(t, p):
                    pe.wait_ge(S["x1_upd"], t + 1)
                    mm(bank[p][:, :], w_pw[:, :], prods[p][:, TAPS - 1, :], stop=False)
                    pe.wait_ge(S["sump_ready"], t + 1)
                    mm(bank[p][:, :], w_pw[:, :], prods[p][:, 0, :], start=False).then_inc(S["pw_ready"], 1)

                for ky in range(3):
                    by_columns(t0, 0, ky)
                for kx in range(3):
                    join_columns(t0, kx)

                def tile1(i, p, seen, left):
                    t = TILES * b + i
                    for k in range(TAPS):
                        if k == 0:
                            pe.wait_ge(S["kl_ready"], t + 1)
                        pe.wait_ge(S["prod1_ready"], TAPS * t + k + 1)
                        mm(bank[4 + k % BC_BANKS][:, :], tap_sel[:, k, :], hl[p][:, :]).then_inc(S["bc_ready"], 1)
                        if left and 2 <= k < 5:
                            by_columns(t + 1, 1 - p, k - 2)
                        if left and k >= 6:
                            join_columns(t + 1, k - 6)
                    if seen:
                        pointwise(t - 1, 1 - p)
                pairs(pe, tile1)
                pe.wait_ge(S["prod1_ready"], TAPS * (t0 + TILES) + BC_BANKS)
                pointwise(t0 + TILES - 1, 1)

                group_norm(2)
                pe.wait_ge(S["late_in"], 16 * 9 * (b + 1))
                pe.wait_ge(S["avg_ready"], b + 1)
                mm(work0[:, 0:1], se_w1, avg).then_inc(S["se1_ps"], 1)
                pe.wait_ge(S["se1_ready"], b + 1)
                mm(work1[:, 0:1], se_w2, se_mid).then_inc(S["se2_ps"], 1)

                def conv(dst, w, p, k, stop):
                    return mm(dst[:, :].rearrange("p (r w) -> p r w", r=ROWS), w[:, k, :],
                              win[p][:, k // 3:k // 3 + ROWS, k % 3:k % 3 + W], start=(k == 0), stop=stop)

                def tile2(i, p, seen, left):
                    t = TILES * b + i
                    pe.wait_ge(S["win2"], t + 1)
                    if seen == 2:
                        pe.wait_ge(S["gated_ready"], t - 1)
                    for k in range(TAPS):
                        m = conv(bank[2 + p], w2, p, k, k == TAPS - 1)
                    m.then_inc(S["conv2_ready"], 1)
                pairs(pe, tile2)

                group_norm(3)

                def spectrum(i, p, seen, left):
                    t = TILES * b + i
                    pe.wait_ge(S["g3_ready"], t + 1)
                    if seen == 2:
                        pe.wait_ge(S["rowt_ready"], t - 1)
                    for r in range(ROWS):
                        m = pe.transpose(bank[2 + p][:, W * r:W * (r + 1)], g_norm[p][:, W * r:W * (r + 1)], ident)
                    m.then_inc(S["rowt_ps"], 1)
                    if seen:
                        dft_rows(t - 1, 1 - p)
                    if not left:
                        dft_rows(t, p)

                def dft_rows(t, p):
                    pe.wait_ge(S["rowt_ready"], t + 1)
                    pe.wait_ge(S["dftw_ready"], t + 1)
                    for r in range(ROWS):
                        m = mm(bank[4 + p][:, 32 * r:32 * (r + 1)], row_t[p][:, W * r:W * (r + 1)], fw)
                    m.then_inc(S["dftw_ps"], 1)
                pairs(pe, spectrum)
                pe.wait_ge(S["dftw_ready"], t0 + TILES + RING)
                for j in range(8):
                    if j >= 2:
                        pe.wait_ge(S["dftt_ready"], 8 * b + j - 1)
                    for f in range(4):
                        m = pe.transpose(bank[2 + j % 2][:, C * f:C * (f + 1)], dft_w[:, :, 4 * j + f], ident)
                    m.then_inc(S["dftt_ps"], 1)
                pe.wait_ge(S["dftt_ready"], 8 * (b + 1))
                for fy in range(MODES):
                    mm(work0[:, 32 * fy:32 * (fy + 1)], dft_wt[:, 2 * fy, :], fh[:, 0:32], stop=False)
                    m = mm(work0[:, 32 * fy:32 * (fy + 1)], dft_wt[:, 2 * fy + 1, :], fh[:, 32:64], start=False)
                m.then_inc(S["spec_ps"], 1)

                def conv3(t, p):
                    pe.wait_ge(S["win3"], t + 1)
                    for k in range(TAPS):
                        conv(bank[4 + p], w3, p, k, False)

                conv3(t0, 0)
                conv3(t0 + 1, 1)
                for k in range(TAPS):
                    pe.wait_ge(S["xt_ready"], TAPS * b + k + 1)
                    for j in range(4):
                        m = mm(o_ps[j][:, 0:C], x_tap[:, k, C * j:C * (j + 1)], w3[:, k, :],
                               start=(k == 0), stop=(k == TAPS - 1))
                m.then_inc(S["o_ps"], 1)

                def low_rows(t, p):
                    pe.wait_ge(S["ta_ready"], t + 1)
                    for j in range(4):
                        m = mm(bank[6 + p][32 * j:32 * (j + 1), 0:C], ta[p], o_t[:, j, :])
                    m.then_inc(S["low_ps"], 1)

                pe.wait_ge(S["o_ready"], b + 1)
                low_rows(t0, 0)

                def tile3(i, p, seen, left):
                    t = TILES * b + i
                    if seen == 2:
                        pe.wait_ge(S["out_ready"], t - 1)
                        conv3(t, p)
                    if left:
                        low_rows(t + 1, 1 - p)
                    pe.wait_ge(S["low_ready"], t + 1)
                    mm(bank[4 + p][:, :], low[p], tab_b, start=False).then_inc(S["conv3_ready"], 1)
                pairs(pe, tile3)

        @block.scalar
        def _(act):
            act.preload_act_table_set(LN_EXP)
            act.wait_ge(S["weights_in"], loaded)
            act.activation(a_neg[:, :, :], a_neg[:, :, :], ACT.Exp).then_inc(S["prep_act"], 1)

            with act.Fori(0, BATCH) as b:
                def group_norm(layer):
                    s = 4 * b + layer + 1
                    act.wait_ge(S["gvar_ps"], s)
                    act.activation(glog, work1[:, 0:1], ACT.Ln, bias=eps_gn).then_inc(S["glog_ready"], 1)
                    act.wait_ge(S["glog_ready"], s)
                    act.activation(grstd, glog, ACT.Exp, scale=-0.5).then_inc(S["grstd_ready"], 1)

                act.preload_act_table_set(LN_EXP)
                group_norm(0)

                def front(t, step):
                    if step == 12:
                        act.wait_ge(S["cen_ready"], t + 1)
                        act.activation(sq, work1[:, :], ACT.Square).then_inc(S["sq_ready"], 1)
                    if step == 14:
                        act.wait_ge(S["var_ready"], t + 1)
                        act.activation(rs, work0[:, :], ACT.Ln, bias=eps_gn).then_inc(S["lnv_ready"], 1)
                        act.wait_ge(S["lnv_ready"], t + 1)
                        act.activation(rs, rs, ACT.Exp, scale=-0.5).then_inc(S["rs_ready"], 1)

                def back(t, r, step, seen=0, start=False):
                    if step == 1:
                        if start:
                            prev = zero3.rearrange("p (h t) -> p h t", h=HALVES)
                        else:
                            act.wait_ge(S["tap_done"], 6 * t)
                            prev = xin[:, :, T:T + 3]
                        act.activation(xin[:, :, 0:3], prev, ACT.Copy).then_inc(S["hist_done"], 1)
                        act.wait_ge(S["hist_done"], t + 1)
                        if seen:
                            act.wait_ge(S["yd_ready"], t - 1)
                        for h in range(HALVES):
                            act.wait_ge(S["xin_ready"], 2 * t + h + 1)
                            src = (work0, work1)[h]
                            act.activation(xin[:, h, 3:T + 3], src[:, :], ACT.Identity, bias=bias_in[:, h:h + 1])
                            act.activation(u[r][:, h, :], src[:, :], ACT.Identity, scale=conv_w[:, h, 3:4],
                                           bias=conv_b3[:, h:h + 1]).then_inc(S["xin_evac"], 1)
                    if step in (3, 4):
                        h = step - 3
                        if h == 0:
                            act.preload_act_table_set(EXP_TANH)
                            if seen:
                                act.wait_ge(S["yz_ready"], t - 1)
                        act.wait_ge(S["z_ready"], 2 * t + h + 1)
                        src = (work0, work1)[h]
                        act.activation(zs[r][:, h, :], src[:, :], ACT.Identity, bias=bias_in[:, 2 + h:3 + h])
                        act.activation(tmp_z[:, h, :], src[:, :], ACT.Tanh,
                                       bias=bias_in[:, 2 + h:3 + h]).then_inc(S["z_evac"], 1)
                    if step == 5:
                        act.wait_ge(S["tap_done"], 6 * (t + 1))
                        act.activation(tmp_u, u[r], ACT.Tanh).then_inc(S["thu_ready"], 1)
                        act.preload_act_table_set(LN_EXP)
                    if step == 8:
                        act.wait_ge(S["xdbl_ready"], t + 1)
                        act.activation(dts, work0[:, :], ACT.Copy).then_inc(S["dts_ready"], 1)
                        act.activation(hl[r][:, :], work0[:, :], ACT.Copy).then_inc(S["hh_ready"], 1)
                    if step == 10:
                        act.wait_ge(S["zs_ready"], t + 1)
                        for h in range(HALVES):
                            act.wait_ge(S["dt_ready"], 2 * t + h + 1)
                            v = (work1, work0)[h]
                            act.activation(tmp_z[:, h, :], v[:, :], ACT.Abs, bias=dt_b[:, h:h + 1])
                            act.activation(delta[r][:, h, :], v[:, :], ACT.Relu,
                                           bias=dt_b[:, h:h + 1]).then_inc(S["v_done"], 1)
                    if step == 11:
                        act.wait_ge(S["v_done"], 2 * t + 2)
                        act.activation(tmp_z, tmp_z, ACT.Exp, scale=-1.0).then_inc(S["exp_done"], 1)
                        act.wait_ge(S["exp_done"], t + 1)
                        act.activation(tmp_z, tmp_z, ACT.Ln, bias=1.0).then_inc(S["sp_ready"], 1)

                def copy_b(t, n):
                    q = DS * t + n
                    act.wait_ge(S["bbc_ready"], q + 1)
                    act.wait_ge(S["dbu_ready"], q + 1)
                    act.activation(b_sb[n % 2], b_ps[n % 2][:, :], ACT.Copy).then_inc(S["bs_ready"], 1)

                def decay(t, r, n):
                    q = DS * t + n
                    if n == 0:
                        act.wait_ge(S["delta_ready"], t + 1)
                    act.wait_ge(S["scan_ready"], q + 1)
                    for h in range(HALVES):
                        a = act.activation(dA[n % DEEP][:, h, :], delta[r][:, h, :], ACT.Exp,
                                           scale=a_neg[:, h, n:n + 1])
                    a.then_inc(S["da_ready"], 1)

                t0 = TILES * b
                act.wait_ge(S["prep_dve"], 4)
                for step in range(DS):
                    front(t0, step)
                for step in range(DS):
                    back(t0, 0, step, start=True)
                    front(t0 + 1, step)
                for n in range(LEAD):
                    copy_b(t0, n)
                    decay(t0, 0, n)
                copy_b(t0, LEAD)

                def tile0(i, p, seen, left):
                    t = TILES * b + i
                    for n in range(DS):
                        ahead = n + LEAD
                        if ahead + 1 < DS:
                            copy_b(t, ahead + 1)
                        elif left:
                            copy_b(t + 1, ahead + 1 - DS)
                        if ahead < DS:
                            decay(t, p, ahead)
                        elif left:
                            decay(t + 1, 1 - p, ahead - DS)
                        if left:
                            back(t + 1, 1 - p, n, seen)
                        if left == 2:
                            front(t + 2, n)
                pairs(act, tile0)

                group_norm(1)

                def head(t, p):
                    act.wait_ge(S["bycol_ps"], t + 1)
                    act.activation(by_column[:, :, 1:W + 1], bank[2][:, :].rearrange("p (r w) -> p r w", r=ROWS),
                                   ACT.Copy).then_inc(S["bycol_ready"], 1)
                    act.wait_ge(S["kern_ready"], t + 1)
                    act.activation(hl[p][:, :], bank[3][:, :], ACT.Identity, bias=b_kg).then_inc(S["kh_ready"], 1)

                head(t0, 0)

                def tile1(i, p, seen, left):
                    if left:
                        head(TILES * b + i + 1, 1 - p)
                pairs(act, tile1)

                group_norm(2)
                act.wait_ge(S["se1_ps"], b + 1)
                act.activation(se_mid, work0[:, 0:1], ACT.Relu).then_inc(S["se1_ready"], 1)
                act.wait_ge(S["se2_ps"], b + 1)
                act.activation(se_exp, work1[:, 0:1], ACT.Exp, scale=-1.0).then_inc(S["seexp_ready"], 1)
                act.wait_ge(S["seb_ready"], b + 1)

                def tile2(i, p, seen, left):
                    t = TILES * b + i
                    act.wait_ge(S["conv2_ready"], t + 1)
                    if seen == 2:
                        act.wait_ge(S["x2_upd"], t - 1)
                    act.activation(gated[p], bank[2 + p][:, :], ACT.Identity, scale=se,
                                   bias=se_b).then_inc(S["gated_ready"], 1)
                pairs(act, tile2)

                group_norm(3)

                def spectrum(i, p, seen, left):
                    t = TILES * b + i
                    act.wait_ge(S["rowt_ps"], t + 1)
                    if seen == 2:
                        act.wait_ge(S["dftw_ps"], t - 1)
                    act.activation(row_t[p], bank[2 + p][:, :], ACT.Copy).then_inc(S["rowt_ready"], 1)
                pairs(act, spectrum)
                for j in range(8):
                    act.wait_ge(S["dftt_ps"], 8 * b + j + 1)
                    act.activation(dft_wt[:, 4 * j:4 * (j + 1), :],
                                   bank[2 + j % 2][:, :].rearrange("p (f c) -> p f c", f=4),
                                   ACT.Copy).then_inc(S["dftt_ready"], 1)
                act.wait_ge(S["o_ps"], b + 1)
                for j in range(4):
                    a = act.activation(o_t[:, j, :], o_ps[j][:, 0:C], ACT.Copy)
                a.then_inc(S["o_ready"], 1)

                def tile3(i, p, seen, left):
                    t = TILES * b + i
                    act.wait_ge(S["low_ps"], t + 1)
                    if seen == 2:
                        act.wait_ge(S["conv3_ready"], t - 1)
                    act.activation(low[p], bank[6 + p][:, 0:C], ACT.Copy).then_inc(S["low_ready"], 1)
                pairs(act, tile3)

        @block.gpsimd
        def _(pool):
            for m in (w_x[:, :, :], w_dt[:, :, :], w_kg[:, :, :], w_pw[:, :]):
                pool.memset(m, 0.0).then_inc(S["prep_pool"], 1)
            pool.memset(ones[:, :], 1.0)
            pool.memset(cols[:, :], 0.0).then_inc(S["prep_pool"], 1)

            with pool.Fori(0, BATCH) as b:
                def input_gain(t, r, start=False):
                    pool.wait_ge(S["delta_ready"], t + 1)
                    if not start:
                        pool.wait_ge(S["dbu_ready"], DS * t + RING)
                    pool.tensor_tensor(du, delta[r], u[r], ALU.mult).then_inc(S["du_ready"], 1)

                def drive(t, n):
                    q = DS * t + n
                    if n == 0:
                        pool.wait_ge(S["du_ready"], t + 1)
                    pool.wait_ge(S["bs_ready"], q + 1 + RING)
                    pool.wait_ge(S["scan_ready"], q + 1)
                    pool.tensor_tensor(dBu[n % DEEP], du, b_sb[n % 2].unsqueeze(1).broadcast_to([C, HALVES, T]),
                                       ALU.mult).then_inc(S["dbu_ready"], 1)

                def save(t, n):
                    pool.wait_ge(S["scan_ready"], DS * t + n + 1 + DEEP)
                    pool.tensor_tensor(state[:, :, n:n + 1], hst[n % 2][:, :, T - 1:T], ones2,
                                       ALU.mult).then_inc(S["st_saved"], 1)

                def gate(t, r):
                    pool.wait_ge(S["yd_ready"], t + 1)
                    pool.wait_ge(S["zs_ready"], t + 1)
                    pool.tensor_tensor(yd, yd, zs[r], ALU.mult).then_inc(S["yz_ready"], 1)

                t0 = TILES * b
                input_gain(t0, 0, start=True)
                for n in range(LEAD):
                    drive(t0, n)

                def tile0(i, p, seen, left):
                    t = TILES * b + i
                    for n in range(DS):
                        ahead = n + LEAD
                        save(t, n)
                        if left and ahead == DS:
                            input_gain(t + 1, 1 - p)
                        if ahead < DS:
                            drive(t, ahead)
                        elif left:
                            drive(t + 1, ahead - DS)
                        if n == 1 and seen:
                            gate(t - 1, 1 - p)
                pairs(pool, tile0)
                gate(t0 + TILES - 1, 1)

                def tile1(i, p, seen, left):
                    t = TILES * b + i
                    pr = prods[p]
                    for half in range(2):
                        pool.wait_ge(S["prod1_ready"], TAPS * t + 4 * (half + 1) + BC_BANKS)
                        lo = 4 * half
                        pool.tensor_tensor(pr[:, lo:lo + 2, :], pr[:, lo:lo + 2, :], pr[:, lo + 2:lo + 4, :],
                                           ALU.add).then_inc(S["addp_done"], 1)
                    pool.wait_ge(S["addp_done"], 3 * t + 2)
                    pool.tensor_tensor(pr[:, 0:2, :], pr[:, 0:2, :], pr[:, 4:6, :],
                                       ALU.add).then_inc(S["addp_done"], 1)
                    pool.wait_ge(S["addp_done"], 3 * t + 3)
                    pool.tensor_tensor(pr[:, 0, :], pr[:, 0, :], pr[:, 1, :], ALU.add).then_inc(S["sump_ready"], 1)
                pairs(pool, tile1)

                pool.wait_ge(S["late_in"], 16 * 9 * (b + 1))
                pool.wait_ge(S["o_ready"], b + 1)

                def tile3(i, p, seen, left):
                    t = TILES * b + i
                    if seen == 2:
                        pool.wait_ge(S["low_ps"], t - 1)
                    pool.tensor_tensor(ta[p], tab_a[:, ds(32 * i, 32)], ones[:, 0:1].broadcast_to([C, 32]),
                                       ALU.mult).then_inc(S["ta_ready"], 1)
                pairs(pool, tile3)

        @block.vector
        def _(dve):
            done = S["prep_dve"]
            dve.wait_ge(S["weights_in"], loaded)
            dve.wait_ge(S["prep_pe"], 1)
            dve.tensor_copy(tap_sel[:, :, :], arena[:, 0:TAPS * C].rearrange("p (k m) -> p k m", k=TAPS))
            dve.tensor_copy(state_sel[:, :], arena[:, 2048:2048 + 2 * DS])
            dve.memset(eps_gn, 1e-5)
            dve.tensor_scalar(w_in[:, 0:2 * C], w_in[:, 0:2 * C], ln_w, None, ALU.mult)
            dve.tensor_scalar(w_in[:, 2 * C:4 * C], w_in[:, 2 * C:4 * C], ln_w, 0.5, ALU.mult, ALU.mult)
            dve.tensor_scalar(bias_in[:, 0:2], work0[:, 0:2], 1.0, None, ALU.mult)
            dve.tensor_scalar(bias_in[:, 2:4], work0[:, 2:4], 0.5, None, ALU.mult)
            dve.tensor_tensor(b_l3, b_l3, b_one, ALU.add)
            dve.tensor_scalar(conv_b, conv_b, 0.5, None, ALU.mult)
            dve.tensor_scalar(conv_w[:, :, :], conv_w[:, :, :], 0.5, None, ALU.mult).then_inc(done, 1)
            dve.wait_ge(done, 1)
            dve.tensor_tensor(conv_b3, conv_w[:, :, 3:4].squeeze(2), bias_in[:, 0:2], ALU.mult).then_inc(done, 1)
            dve.wait_ge(done, 2)
            dve.tensor_tensor(conv_b3, conv_b3, conv_b, ALU.add).then_inc(done, 1)
            dve.wait_ge(S["prep_act"], 1)
            dve.tensor_scalar(a_neg[:, :, :], a_neg[:, :, :], -1.0, None, ALU.mult).then_inc(done, 1)
            dve.wait_ge(done, 4)

            with dve.Fori(0, BATCH) as b:
                def tile_stats(i):
                    dve.bn_stats(stats[:, ds(i, 1), :].rearrange("p a s -> p (a s)"), px(i)).then_inc(S["stats_done"], 1)

                def group_norm(layer):
                    s = 4 * b + layer + 1
                    dve.wait_ge(S["stats_done"], TILES * s)
                    dve.memset(spare, 0.0)
                    dve.bn_aggr(mv, stats[:, :, :].rearrange("p t s -> p (t s)")).then_inc(S["mv_ready"], 1)
                    dve.wait_ge(S["mv_ready"], s)
                    dve.wait_ge(S["gmean_ps"], s)
                    dve.tensor_copy(gmean, work0[:, 0:1]).then_inc(S["gmean_ready"], 1)
                    dve.wait_ge(S["gmean_ready"], 2 * s - 1)
                    dve.tensor_tensor(dmean, mv[:, 0:1], gmean, ALU.subtract).then_inc(S["gmean_ready"], 1)
                    dve.wait_ge(S["gmean_ready"], 2 * s)
                    dve.scalar_tensor_tensor(out=gvar, in0=dmean, scalar=dmean, in1=mv[:, 1:2], op0=ALU.mult,
                                             op1=ALU.add).then_inc(S["gvar_ready"], 1)
                    dve.wait_ge(S["grstd_ready"], s)

                def normalise(dst, src):
                    return dve.tensor_scalar(dst, src, gmean, grstd, ALU.subtract, ALU.mult)

                def window(i, p, counter):
                    normalise(win[p][:, :, 1:W + 1],
                              px(i, 6, 1).rearrange("p (r w) -> p r w", r=6)).then_inc(S[counter], 1)

                def pad_rows(layer):
                    for r in (0, H + 1):
                        dve.tensor_scalar(xres[:, W * r:W * (r + 1)], ident, 0.0, gmean, ALU.mult,
                                          ALU.add).then_inc(S["pads_done"], 1)
                    dve.wait_ge(S["pads_done"], 6 * b + 2 * layer)

                for k in range(8):
                    dve.wait_ge(x_in[k], 16 * (b + 1))
                    for j in range(4):
                        tile_stats(4 * k + j)

                group_norm(0)

                def taps(t, r, k):
                    for h in range(HALVES):
                        if k < 2:
                            dve.wait_ge(S["tap_done"], 6 * t + 2 * (2 - k) - 1 + h)
                        dve.scalar_tensor_tensor(out=u[r][:, h, :], in0=xin[:, h, k:k + T],
                                                 scalar=conv_w[:, h, k:k + 1], in1=u[r][:, h, :],
                                                 op0=ALU.mult, op1=ALU.add).then_inc(S["tap_done"], 1)

                def front(t, i, step, first=False):
                    if step == 10:
                        if not first:
                            dve.wait_ge(S["u_ready"], t)
                        normalise(g_tile, px(i)).then_inc(S["g_ready"], 1)
                    if step == 15:
                        dve.wait_ge(S["rs_ready"], t + 1)
                        dve.tensor_tensor(xn, work1[:, :], rs, ALU.mult).then_inc(S["xn_ready"], 1)

                def back(t, r, step):
                    if step in (2, 3, 4):
                        if step == 2:
                            dve.wait_ge(S["xin_evac"], 2 * t + 2)
                        taps(t, r, 4 - step)
                    if step == 5:
                        dve.wait_ge(S["z_evac"], 2 * t + 2)
                        dve.scalar_tensor_tensor(out=zs[r], in0=tmp_z, scalar=1.0, in1=zs[r], op0=ALU.add,
                                                 op1=ALU.mult).then_inc(S["zs_ready"], 1)
                    if step == 6:
                        dve.wait_ge(S["thu_ready"], t + 1)
                        dve.scalar_tensor_tensor(out=u[r], in0=tmp_u, scalar=1.0, in1=u[r], op0=ALU.add,
                                                 op1=ALU.mult).then_inc(S["u_ready"], 1)
                    if step == 9:
                        dve.wait_ge(S["hh_ready"], t + 1)
                        dve.tensor_tensor(hl[r][64:96, :], dts[64:96, :], hl[r][64:96, :].bitcast(F32),
                                          ALU.subtract).then_inc(S["l_ready"], 1)
                    if step == 12:
                        dve.wait_ge(S["sp_ready"], t + 1)
                        dve.tensor_tensor(delta[r], delta[r], tmp_z, ALU.add).then_inc(S["delta_ready"], 1)

                def post(t, i, r, step):
                    if step == 0:
                        dve.wait_ge(S["prod_used"], DS * (t + 1) + DEEP)
                        for h in range(HALVES):
                            a = dve.scalar_tensor_tensor(out=yd[:, h, :], in0=u[r][:, h, :],
                                                         scalar=d_skip[:, h:h + 1], in1=y_ps[h][:, :],
                                                         op0=ALU.mult, op1=ALU.add)
                        a.then_inc(S["yd_ready"], 1)
                    if step == 6:
                        dve.wait_ge(S["proj_ready"], t + 1)
                        dve.tensor_tensor(px(i), work0[:, :], px(i), ALU.add).then_inc(S["x0_upd"], 1)
                    if step == 8:
                        dve.wait_ge(S["x0_upd"], t + 1)
                        tile_stats(i)

                def scan(t, n, start):
                    q = DS * t + n
                    dve.wait_ge(S["da_ready"], q + 1)
                    dve.wait_ge(S["dbu_ready"], q + 1 + RING)
                    dve.wait_ge(S["st_saved"], q + 1)
                    dve.wait_ge(S["prod_ready"], q + 1)
                    for h in range(HALVES):
                        a = dve.tensor_tensor_scan(hst[n % 2][:, h, :], dA[n % DEEP][:, h, :], dBu[n % DEEP][:, h, :],
                                                   0.0 if start else state[:, h, n:n + 1], ALU.mult, ALU.add)
                    a.then_inc(S["scan_ready"], 1)

                def read_out(t, n):
                    q = DS * t + n
                    dve.wait_ge(S["scan_ready"], q + 1 + DEEP)
                    dve.wait_ge(S["cbc_ready"], q + 1)
                    dve.wait_ge(S["prod_used"], q + 1)
                    dve.tensor_tensor(prod[n % DEEP], hst[n % 2], c_ps[n % 2][:, :].unsqueeze(1).broadcast_to(
                        [C, HALVES, T]), ALU.mult).then_inc(S["prod_ready"], 1)

                t0 = TILES * b
                for step in range(DS):
                    front(t0, 0, step, first=True)
                for step in range(DS):
                    back(t0, 0, step)
                    front(t0 + 1, 1, step)
                scan(t0, 0, True)

                def tile0(i, p, seen, left):
                    t = TILES * b + i
                    for n in range(DS):
                        if n + 1 < DS:
                            scan(t, n + 1, not seen)
                        elif left:
                            scan(t + 1, 0, False)
                        read_out(t, n)
                        if left:
                            back(t + 1, 1 - p, n)
                        if seen:
                            post(t - 1, i - 1, 1 - p, n)
                        if left == 2:
                            front(t + 2, i + 2, n)
                pairs(dve, tile0)
                for step in range(DS):
                    post(t0 + TILES - 1, TILES - 1, 1, step)

                group_norm(1)
                pad_rows(1)
                for p in range(2):
                    dve.memset(win[p][:, :, 0:1], 0.0)
                    dve.memset(win[p][:, :, W + 1:W + 2], 0.0)
                dve.memset(by_column[:, :, 0:1], 0.0)
                dve.memset(by_column[:, :, W + 1:W + 2], 0.0)

                def rest(t, p):
                    dve.wait_ge(S["kh_ready"], t + 1)
                    dve.scalar_tensor_tensor(out=hl[p][64:128, :], in0=bank[3][64:128, :],
                                             scalar=b_kg[64:128, :], in1=hl[p][64:128, :].bitcast(F32),
                                             op0=ALU.add, op1=ALU.subtract).then_inc(S["kl_ready"], 1)

                def update1(t, i, p):
                    dve.wait_ge(S["pw_ready"], t + 1)
                    dve.scalar_tensor_tensor(out=px(i), in0=bank[p][:, :], scalar=b_pw, in1=px(i),
                                             op0=ALU.add, op1=ALU.add).then_inc(S["x1_upd"], 1)

                def stats1(t, i):
                    dve.wait_ge(S["x1_upd"], t + 1 + RING)
                    tile_stats(i)

                window(0, 0, "win1")
                rest(t0, 0)

                def tile1(i, p, seen, left):
                    t = TILES * b + i
                    if left:
                        dve.wait_ge(S["prod1_ready"], TAPS * t + BC_BANKS)
                        window(i + 1, 1 - p, "win1")
                    if seen == 2:
                        dve.wait_ge(S["pw_ready"], t - 1)
                    for k in range(TAPS):
                        dve.wait_ge(S["bc_ready"], TAPS * t + k + 1)
                        dve.tensor_tensor(prods[p][:, k, :].rearrange("p (r w) -> p r w", r=ROWS),
                                          bank[4 + k % BC_BANKS][:, :].rearrange("p (r w) -> p r w", r=ROWS),
                                          win[p][:, k // 3:k // 3 + ROWS, k % 3:k % 3 + W],
                                          ALU.mult).then_inc(S["prod1_ready"], 1)
                        if k == 2 and seen == 2:
                            update1(t - 2, i - 2, p)
                        if k == 5 and seen == 2:
                            stats1(t - 2, i - 2)
                    if left:
                        rest(t + 1, 1 - p)
                pairs(dve, tile1)
                for back_to in (2, 1):
                    i = TILES - back_to
                    update1(t0 + i, i, i % 2)
                    stats1(t0 + i, i)

                group_norm(2)
                pad_rows(2)
                dve.tensor_tensor(avg, dmean, grstd, ALU.mult).then_inc(S["avg_ready"], 1)
                dve.wait_ge(S["seexp_ready"], b + 1)
                dve.tensor_scalar(se, se_exp, 1.0, None, ALU.add).then_inc(S["seadd_ready"], 1)
                dve.wait_ge(S["seadd_ready"], b + 1)
                dve.reciprocal(se, se).then_inc(S["se_ready"], 1)
                dve.wait_ge(S["se_ready"], b + 1)
                dve.tensor_tensor(se_b, b_e, se, ALU.mult).then_inc(S["seb_ready"], 1)

                def update2(t, i, p):
                    dve.wait_ge(S["gated_ready"], t + 1)
                    dve.tensor_tensor(px(i), gated[p], px(i), ALU.add).then_inc(S["x2_upd"], 1)
                    dve.wait_ge(S["x2_upd"], t + 1)
                    tile_stats(i)

                window(0, 0, "win2")

                def tile2(i, p, seen, left):
                    t = TILES * b + i
                    if left:
                        if seen:
                            dve.wait_ge(S["conv2_ready"], t)
                        window(i + 1, 1 - p, "win2")
                    if seen:
                        dve.wait_ge(S["win2"], t + (2 if left else 1))
                        update2(t - 1, i - 1, 1 - p)
                pairs(dve, tile2)
                update2(t0 + TILES - 1, TILES - 1, 1)

                group_norm(3)
                pad_rows(3)

                def spectrum(i, p, seen, left):
                    t = TILES * b + i
                    if left:
                        if seen:
                            dve.wait_ge(S["rowt_ps"], t)
                        normalise(g_norm[1 - p], px(i + 1)).then_inc(S["g3_ready"], 1)
                    if seen:
                        keep_rows(t - 1, i - 1, 1 - p)
                    if not left:
                        keep_rows(t, i, p)

                def keep_rows(t, i, p):
                    dve.wait_ge(S["dftw_ps"], t + 1)
                    dve.tensor_copy(dft_w[:, ds(ROWS * i, ROWS), :],
                                    bank[4 + p][:, 0:32 * ROWS].rearrange("p (h f) -> p h f", h=ROWS)
                                    ).then_inc(S["dftw_ready"], 1)
                normalise(g_norm[0], px(0)).then_inc(S["g3_ready"], 1)
                pairs(dve, spectrum)
                window(0, 0, "win3")
                window(1, 1, "win3")

                def rotate(dst, src, axis, k):
                    cos, sin = (rot[:, T * (2 * axis + a):T * (2 * axis + a + 1)] for a in range(2))
                    x4, s4, r4 = (v.rearrange("p (y r x) -> p y r x", y=MODES, r=2) for v in (src, sin, rot_tmp))
                    q = (TAPS - 1) * b + k
                    for r in range(2):
                        a = dve.tensor_tensor(r4[:, :, r, :], x4[:, :, 1 - r, :], s4[:, :, r, :], ALU.mult)
                    dve.tensor_tensor(dst, src, cos, ALU.mult).then_inc(S["rot1_done"], 1)
                    dve.wait_ge(S["rot1_done"], q)
                    dve.tensor_tensor(dst, dst, rot_tmp, ALU.add).then_inc(S["xt_ready"], 1)

                dve.wait_ge(S["spec_ps"], b + 1)
                dve.tensor_copy(x_tap[:, 0, :], work0[:, :]).then_inc(S["xt_ready"], 1)
                for k in range(1, TAPS):
                    axis, of = (1, k - 1) if k % 3 else (0, k - 3)
                    dve.wait_ge(S["xt_ready"], TAPS * b + k)
                    rotate(x_tap[:, k, :], x_tap[:, of, :], axis, k)

                def store_tile(t, i, p):
                    dve.wait_ge(S["conv3_ready"], t + 1)
                    dve.wait_ge(stored[p], 8 * (t - p) + 16)
                    dve.scalar_tensor_tensor(out=out_buf[p], in0=bank[4 + p][:, :], scalar=b_l3, in1=px(i),
                                             op0=ALU.add, op1=ALU.add).then_inc(S["out_ready"], 1)

                def tile3(i, p, seen, left):
                    t = TILES * b + i
                    if left and seen:
                        dve.wait_ge(S["conv3_ready"], t)
                        window(i + 1, 1 - p, "win3")
                    if seen:
                        store_tile(t - 1, i - 1, 1 - p)
                pairs(dve, tile3)
                store_tile(t0 + TILES - 1, TILES - 1, 1)


_SHAPE = (BATCH, C, H, W)


def kernel(**inputs):
    from concourse import bacc
    from concourse.bass_utils import run_bass_kernel_spmd

    x = {k: np.asarray(v) for k, v in inputs.items()}

    def halves(a):
        return a.reshape(HALVES, C, -1).transpose(1, 0, 2)

    def column(a):
        return a.reshape(-1, 1)

    def taps(a):
        return a.reshape(a.shape[0], a.shape[1], TAPS).transpose(1, 2, 0)

    arrays = {
        "x": x["x"].reshape(BATCH, C, H * W),
        "w_in": x["L0_conv_W_in"].T, "w_x": halves(x["L0_conv_W_xproj"].T),
        "w_dt": x["L0_conv_W_dt"].T.reshape(8, HALVES, C), "w_out": halves(x["L0_conv_W_out"].T),
        "a_log": halves(x["L0_conv_A_log"]), "conv_w": halves(x["L0_conv_conv_w"]),
        "ln_w": column(x["L0_conv_ln_w"]), "ln_b": column(x["L0_conv_ln_b"]),
        "conv_b": x["L0_conv_conv_b"].reshape(HALVES, C).T, "b_dt": x["L0_conv_b_dt"].reshape(HALVES, C).T,
        "d": x["L0_conv_D"].reshape(HALVES, C).T,
        "w_kg": x["L1_conv_w_kg"].reshape(4, TAPS, 32, 3, 3).transpose(0, 4, 2, 3, 1),
        "b_kg": column(x["L1_conv_b_kg"]), "w_pw": x["L1_conv_w_pw"].reshape(4, 32, 32).transpose(0, 2, 1),
        "b_pw": column(x["L1_conv_b_pw"]),
        "w2": taps(x["L2_conv_weight"][0]), "b_e": column(x["L2_conv_bias_e"][0]),
        "se_w1": np.pad(x["L2_conv_se_w1"].T, ((0, 0), (0, C - 16))),
        "se_w2": np.pad(x["L2_conv_se_w2"].T, ((0, C - 16), (0, 0))),
        "w3": taps(x["L3_conv_weight"]), "b_l3": column(x["L3_conv_conv_bias"]),
        "b_one": x["L3_conv_bias"].reshape(1, 1),
        **{k: v.astype(np.float32) for k, v in shape_tables().items()},
    }
    arrays = {f"in_{k}": np.ascontiguousarray(v) for k, v in arrays.items()}
    nc = bacc.Bacc("TRN2", target_bir_lowering=False, num_devices=1)
    io = {k[3:]: nc.dram_tensor(k, v.shape, F32, kind="ExternalInput").ap() for k, v in arrays.items()}
    out = nc.dram_tensor("out", (BATCH, C, H * W), F32, kind="ExternalOutput").ap()
    build(nc, io, out)
    done = run_bass_kernel_spmd(nc, [arrays], core_ids=[0])
    return done.results[0]["out"].reshape(_SHAPE)
```

```python
from contextlib import ExitStack

import numpy as np

import concourse.bass as bass
from concourse import mybir
from concourse.bass import ds

F32 = mybir.dt.float32
F32R = mybir.dt.float32r
ALU = mybir.AluOpType
ACT = mybir.ActivationFunctionType

BATCH, C, H, W = 4, 128, 128, 128
ROWS = 4
T = ROWS * W
TILES = H // ROWS
HALVES = 2
DS = 16
TAPS = 9
KERNELS = 4 * TAPS
MODES = 16
RING = 2
DEEP = 4
LEAD = 3
BC_BANKS = 3
PADW = W + 2
LN_EXP = "natural_log_exp_and_others"
EXP_TANH = "exp_and_others"


def shape_tables():
    f = np.float64
    eye = np.eye(C, dtype=f)
    mean = np.full((C, C), 1.0 / C)
    group = np.kron(np.eye(C // 4), np.full((4, 4), 0.25))
    state_sel = np.zeros((C, 2 * DS))
    for n in range(2 * DS):
        state_sel[32 + n, n] = state_sel[64 + n, n] = 1.0
    kernel_sel = np.zeros((C, KERNELS))
    for m in range(KERNELS):
        kernel_sel[m, m] = kernel_sel[64 + m, m] = 1.0
    shift_sel = np.zeros((C, 3, C))
    for kx in range(3):
        for m in range(KERNELS):
            shift_sel[KERNELS * kx + m, kx, m] = shift_sel[KERNELS * kx + m, kx, 64 + m] = 1.0
    two_pi = 2 * np.pi / W
    w, fr, hh = np.arange(W), np.arange(MODES), np.arange(H)
    fw = np.zeros((W, MODES, 2))
    fw[:, :, 0], fw[:, :, 1] = np.cos(two_pi * np.outer(w, fr)), -np.sin(two_pi * np.outer(w, fr))
    cos_h, sin_h = np.cos(two_pi * np.outer(hh, fr)), np.sin(two_pi * np.outer(hh, fr))
    fh = np.stack([np.stack([cos_h, -sin_h], 1), np.stack([sin_h, cos_h], 1)], 1)
    rot = np.zeros((2, 2, MODES, 2, MODES))
    for axis, phase in ((0, fr[None, :] + 0 * fr[:, None]), (1, fr[:, None] + 0 * fr[None, :])):
        for r in range(2):
            rot[axis, 0, :, r, :] = np.cos(two_pi * phase)
            rot[axis, 1, :, r, :] = (1, -1)[r] * np.sin(two_pi * phase)
    ta = np.zeros((4, 2, MODES, TILES, ROWS, 4, 2))
    for fy in range(4):
        c, s = (np.transpose(v.reshape(TILES, ROWS, MODES), (2, 0, 1)) for v in (cos_h, sin_h))
        ta[fy, 0, :, :, :, fy, 0], ta[fy, 1, :, :, :, fy, 0] = c, -s
        ta[fy, 0, :, :, :, fy, 1], ta[fy, 1, :, :, :, fy, 1] = s, c
    tb = np.zeros((4, ROWS, 4, 2, ROWS, W))
    for j in range(4):
        for r in range(ROWS):
            for fy in range(4):
                ph = two_pi * (4 * j + fy) * w
                tb[j, r, fy, 0, r], tb[j, r, fy, 1, r] = np.cos(ph) / (H * W), -np.sin(ph) / (H * W)
    return {
        "t_square": np.stack([eye, eye - mean, mean, group], 1).reshape(C, 4 * C),
        "t_state_sel": state_sel, "t_kernel_sel": kernel_sel,
        "t_shift_sel": shift_sel.reshape(C, 3 * C),
        "t_fw": fw.reshape(W, 32), "t_fh": fh.reshape(H, 64), "t_rot": rot.reshape(1, -1),
        "t_ta": ta.reshape(C, TILES * 32), "t_tb": tb.reshape(C, T),
    }


def build(nc, io, out):
    ctx = ExitStack()
    with ctx:
        def sb(name, shape, dt=F32):
            return ctx.enter_context(nc.sbuf_tensor(name, shape, dt))

        def sem(name):
            return ctx.enter_context(nc.semaphore(name))

        xres = sb("xres", [C, (H + 2) * W])
        square = sb("square", [C, 4 * C])
        ident, center, meanmat, groupmat = (square[:, C * k:C * (k + 1)] for k in range(4))
        state_sel = sb("state_sel", [C, 2 * DS], F32R)
        kernel_sel = sb("kernel_sel", [C, KERNELS])
        hl = [sb(f"hl{p}", [C, T], F32R) for p in range(2)]
        w_in = sb("w_in", [C, 4 * C])
        w_x = sb("w_x", [C, HALVES, C])
        w_dt = sb("w_dt", [C, HALVES, C])
        w_out = sb("w_out", [C, HALVES, C])
        w_skip = sb("w_skip", [C, HALVES, C])
        w_kg = sb("w_kg", [C, 3, C])
        shift_sel = sb("shift_sel", [C, 3, C])
        w_pw = sb("w_pw", [C, C])
        a_neg = sb("a_neg", [C, HALVES, DS])
        state = sb("state", [C, HALVES, DS])
        conv_w = sb("conv_w", [C, HALVES, 4])
        cols = sb("cols", [C, 40])
        (ln_w, ln_b, eps_gn, b_kg, b_pw, b_e, b_l3, b_one) = (cols[:, k:k + 1] for k in range(8))
        bias_in, conv_b, dt_b, d_skip = (cols[:, 8:12], cols[:, 12:14], cols[:, 14:16], cols[:, 16:18])
        conv_b3, gmean, grstd, dmean, gvar, se, se_b = (
            cols[:, 18:20], cols[:, 20:21], cols[:, 21:22], cols[:, 22:23], cols[:, 23:24],
            cols[:, 24:25], cols[:, 25:26])
        avg, se_mid, se_exp, glog, mv = (
            cols[:, 26:27], cols[:, 27:28], cols[:, 28:29], cols[:, 29:30], cols[:, 30:32])
        zero3, spare, gshift = cols[:, 32:38], cols[:, 38:39], cols[:, 39:40]
        ones = sb("ones", [C, HALVES])
        ones2 = ones[:, :].unsqueeze(2)
        stats = sb("stats", [C, TILES, 6])

        def carve(tensor):
            at = [0]

            def take(n):
                at[0] += n
                assert at[0] <= tensor.shape[1]
                return tensor[:, at[0] - n:at[0]]
            return take

        scan_cols = HALVES * (T + 1)
        arena0_cols = (2 * T + HALVES * (T + 3) + 10 * HALVES * T + 3 * DEEP * scan_cols
                       + DEEP * HALVES * T + DEEP * T)
        with nc.sbuf_tensor("arena0", [C, arena0_cols], F32) as arena0:
            take = carve(arena0)

        def halves(n=T):
            return take(HALVES * n).rearrange("p (h t) -> p h t", h=HALVES)

        xin, tmp_z, tmp_u, du, yd = halves(T + 3), halves(), halves(), halves(), halves()
        g_tile, sq, rs = tmp_u[:, 0, :], tmp_u[:, 1, :], tmp_u[:, 0, :]
        xn, dts = take(T), take(T)
        u, zs, delta = ([halves() for _ in range(2)] for _ in range(3))
        dA, dBu, hst = ([halves(1 + T) for _ in range(DEEP)] for _ in range(3))
        prod = [halves() for _ in range(DEEP)]
        b_sb = [take(T) for _ in range(DEEP)]

        arena = sb("arena", [C, 24760])
        take = carve(arena)
        w2 = take(TAPS * C).rearrange("p (k o) -> p k o", k=TAPS)
        w3 = take(TAPS * C).rearrange("p (k o) -> p k o", k=TAPS)
        se_w1, se_w2 = take(C), take(C)
        tab_a = take(TILES * 32)
        tab_b = take(T)
        fw, fh, rot = take(32), take(64), take(4 * 512)
        win = [take(6 * PADW).rearrange("p (r w) -> p r w", r=6) for _ in range(2)]
        out_buf = [take(T) for _ in range(2)]
        gated = [take(T) for _ in range(2)]
        by_column = take(ROWS * PADW).rearrange("p (r w) -> p r w", r=ROWS)
        over = take(4608)
        prods = [over.rearrange("p (k t) -> p k t", k=TAPS)]
        row_t = [over[:, T * k:T * (k + 1)] for k in range(2)]
        g_norm = [over[:, T * (k + 2):T * (k + 3)] for k in range(2)]
        over = take(4608)
        dft_w = over[:, 0:4096].rearrange("p (h f) -> p h f", h=H)
        x_tap = over.rearrange("p (k f) -> p k f", k=TAPS)
        prods.append(over.rearrange("p (k t) -> p k t", k=TAPS))
        dft_wt = take(4096).rearrange("p (f c) -> p f c", f=32)
        rot_tmp = gated[0]
        o_t = take(T).rearrange("p (j k) -> p j k", j=4)
        ta = [take(32) for _ in range(2)]
        low = [take(C) for _ in range(2)]

        w_hl = [sb(f"w_hl{k}", [C, TAPS, C], F32R) for k in range(2)]
        tap_sel = w_hl[0]
        win_hl = [[sb(f"win_hl{p}{k}", [C, 6, PADW], F32R) for k in range(2)] for p in range(2)]

        bank = [ctx.enter_context(nc.psum_tensor(f"bank{k}", [C, T], F32)) for k in range(8)]
        work0, work1 = bank[0], bank[1]
        b_ps, c_ps, y_ps = bank[2:4], bank[4:6], bank[6:8]
        o_ps = bank[1:4] + bank[6:7]

        names = """weights_in late_in prep_pool prep_dve prep_pe prep_act
            stats_done mv_ready gmean_ps gmean_ready gvar_ready gvar_ps glog_ready grstd_ready
            gshift_ready g_ready cen_ready sq_ready var_ready lnv_ready rs_ready xn_ready xin_ready xin_evac hist_done
            z_ready z_evac zs_ready tap_done thu_ready u_ready xdbl_ready dts_ready hh_ready l_ready
            dt_ready v_done exp_done sp_ready delta_ready du_ready
            bbc_ready bs_ready dbu_ready da_ready scan_ready st_saved cbc_ready prod_ready prod_used
            y_ready yz_ready proj_ready x0_upd
            selectors win1 bycol_ps bycol_ready kern_ready kh_ready kl_ready bc_ready prod1_ready addp_done
            sump_ready pw_ready x1_upd
            avg_ready se1_ps se1_ready se2_ps seexp_ready seadd_ready se_ready seb_ready
            w_rounded w_split win2 rounded2 split2 conv2_ready gated_ready x2_upd
            g3_ready rowt_ps rowt_ready dftw_ps dftw_ready dftt_ps dftt_ready spec_ps
            xt_ready rot1_done o_ps o_ready ta_ready low_ps low_ready
            win3 rounded3 split3 conv3_ready out_ready pads_done""".split()
        S = {n: sem(n) for n in names}
        x_first = [sem(f"x_first{k}") for k in range(8)]
        x_in = [sem(f"x_in{p}") for p in range(2)]
        stored = [sem(f"stored{p}") for p in range(2)]

        def px(i, rows=ROWS, up=0):
            return xres[:, ds(W * (1 - up) + T * i, rows * W)]

        def pairs(eng, tile):
            tile(0, 0, 0, 2)
            tile(1, 1, 1, 2)
            with eng.Fori(1, TILES // 2 - 1) as k:
                tile(2 * k, 0, 2, 2)
                tile(2 * k + 1, 1, 2, 2)
            tile(TILES - 2, 0, 2, 1)
            tile(TILES - 1, 1, 2, 0)

        loads = [
            (square[:, :], io["t_square"]), (shift_sel[:, :, :].rearrange("p k m -> p (k m)"), io["t_shift_sel"]), (w_in[:, :], io["w_in"]),
            (w_x[:, :, 0:8], io["w_x"][:, :, 0:8]), (w_x[:, :, 32:64], io["w_x"][:, :, 8:40]),
            (w_x[:, :, 64:96], io["w_x"][:, :, 8:40]), (w_dt[0:8, :, :], io["w_dt"]),
            (w_out[:, :, :], io["w_out"]), (a_neg[:, :, :], io["a_log"]),
            (conv_w[:, :, :], io["conv_w"]), (ln_w, io["ln_w"]), (ln_b, io["ln_b"]),
            (conv_b, io["conv_b"]), (dt_b, io["b_dt"]), (d_skip, io["d"]),
            (b_kg[0:36, :], io["b_kg"]), (b_kg[64:100, :], io["b_kg"]), (b_pw, io["b_pw"]),
            (b_e, io["b_e"]), (b_l3, io["b_l3"]), (b_one, io["b_one"].partition_broadcast(C)),
            (kernel_sel[:, :], io["t_kernel_sel"]), (arena[:, C:C + 2 * DS], io["t_state_sel"]),
        ]
        for g in range(4):
            lo = 32 * g
            for kx in range(3):
                at_kx = KERNELS * kx + TAPS * g
                loads.append((w_kg[lo:lo + 32, :, at_kx:at_kx + TAPS], io["w_kg"][g, kx]))
            loads.append((w_pw[lo:lo + 32, lo:lo + 32], io["w_pw"][g]))
        loaded = 16 * len(loads)

        block = ctx.enter_context(nc.Block())

        @block.sync
        def _(sp):
            for name in ("bs_ready", "prod_ready", "dftw_ready",
                         "x1_upd"):
                sp.sem_inc(S[name], RING)
            for name in ("scan_ready", "prod_used", "st_saved", "dbu_ready"):
                sp.sem_inc(S[name], DEEP)
            sp.sem_inc(S["prod1_ready"], BC_BANKS)
            for p in range(2):
                sp.sem_inc(stored[p], 16)
                sp.sem_inc(x_in[p], 16)
            sp.wait_ge(S["prep_pool"], 5)
            for dst, src in loads:
                sp.dma_start(dst, src).then_inc(S["weights_in"], 16)
            for k in range(8):
                sp.dma_start(xres[:, W + 2048 * k:W + 2048 * (k + 1)],
                             io["x"][0, :, 2048 * k:2048 * (k + 1)]).then_inc(x_first[k], 16)

            def image(b, more):
                sp.wait_ge(S["x0_upd"], TILES * (b + 1))
                for dst, src in ((w2, io["w2"]), (w3, io["w3"]), (se_w1, io["se_w1"]), (se_w2, io["se_w2"]),
                                 (tab_a, io["t_ta"]), (tab_b, io["t_tb"]), (fw, io["t_fw"]), (fh, io["t_fh"]),
                                 (rot, io["t_rot"].partition_broadcast(C))):
                    sp.dma_start(dst, src).then_inc(S["late_in"], 16)

                def store(i, p, seen, left):
                    sp.wait_ge(S["out_ready"], TILES * b + i + 1)
                    sp.dma_start(out[ds(b, 1), :, ds(T * i, T)].rearrange("b c t -> (b c) t"),
                                 out_buf[p]).then_inc(stored[p], 16)
                    if more:
                        sp.wait_ge(x_in[p], 8 * (TILES * b + i - p) + 16)
                        sp.dma_start(px(i), io["x"][ds(b + 1, 1), :, ds(T * i, T)].rearrange("b c t -> (b c) t")
                                     ).then_inc(x_in[p], 16)
                    else:
                        sp.sem_inc(x_in[p], 16)
                pairs(sp, store)

            with sp.Fori(0, BATCH - 1) as b:
                image(b, True)
            image(BATCH - 1, False)
            for p in range(2):
                sp.wait_ge(stored[p], 16 * (TILES // 2) * BATCH + 16)

        @block.tensor
        def _(pe):
            def mm(dst, lhs, rhs, start=True, stop=True):
                return pe.matmul(dst, lhs, rhs, start=start, stop=stop)

            pe.wait_ge(S["weights_in"], loaded)
            for k in range(4):
                last_mm = mm(work0[:, k:k + 1], w_in[:, C * k:C * (k + 1)], ln_b)
            last_mm.then_inc(S["prep_pe"], 1)
            pe.wait_ge(S["prep_dve"], 4)

            with pe.Fori(0, BATCH) as b:
                def group_norm(layer):
                    s = 4 * b + layer + 1
                    pe.wait_ge(S["mv_ready"], s)
                    mm(work0[:, 0:1], groupmat, mv[:, 0:1]).then_inc(S["gmean_ps"], 1)
                    pe.wait_ge(S["gvar_ready"], s)
                    mm(work1[:, 0:1], groupmat, gvar).then_inc(S["gvar_ps"], 1)

                group_norm(0)

                def front(t, step, first=False):
                    if step == 11:
                        pe.wait_ge(S["g_ready"], t + 1)
                        if not first:
                            pe.wait_ge(S["v_done"], 2 * t)
                        mm(work1[:, :], center, g_tile).then_inc(S["cen_ready"], 1)
                    if step == 13:
                        pe.wait_ge(S["sq_ready"], t + 1)
                        mm(work0[:, :], meanmat, sq).then_inc(S["var_ready"], 1)

                def back(t, r, step, seen=0):
                    if step == 0:
                        pe.wait_ge(S["xn_ready"], t + 1)
                        mm(work0[:, :], w_in[:, 0:C], xn).then_inc(S["xin_ready"], 1)
                        mm(work1[:, :], w_in[:, C:2 * C], xn).then_inc(S["xin_ready"], 1)
                    if step == 2:
                        pe.wait_ge(S["xin_evac"], 2 * t + 1)
                        mm(work0[:, :], w_in[:, 2 * C:3 * C], xn).then_inc(S["z_ready"], 1)
                    if step == 3:
                        pe.wait_ge(S["xin_evac"], 2 * t + 2)
                        mm(work1[:, :], w_in[:, 3 * C:4 * C], xn).then_inc(S["z_ready"], 1)
                    if step == 6:
                        pe.wait_ge(S["z_evac"], 2 * t + 1)
                        pe.wait_ge(S["u_ready"], t + 1)
                        mm(work0[:, :], w_x[:, 0, :], u[r][:, 0, :], stop=False)
                        mm(work0[:, :], w_x[:, 1, :], u[r][:, 1, :], start=False).then_inc(S["xdbl_ready"], 1)
                    if step == 8:
                        pe.wait_ge(S["z_evac"], 2 * t + 2)
                        if seen:
                            pe.wait_ge(S["x0_upd"], t - 1)
                        pe.wait_ge(S["dts_ready"], t + 1)
                        mm(work1[:, :], w_dt[:, 0, :], dts).then_inc(S["dt_ready"], 1)
                        pe.wait_ge(S["hh_ready"], t + 1)
                        mm(work0[:, :], w_dt[:, 1, :], dts).then_inc(S["dt_ready"], 1)

                def post(t, left):
                    if left:
                        pe.wait_ge(S["z_evac"], 2 * t + 6)
                    pe.wait_ge(S["yz_ready"], t + 1)
                    mm(work1[:, :], w_out[:, 0, :], yd[:, 0, :], stop=False)
                    mm(work1[:, :], w_out[:, 1, :], yd[:, 1, :], start=False).then_inc(S["proj_ready"], 1)

                def bcast_b(t, r, n):
                    q = DS * t + n
                    if n == 0:
                        pe.wait_ge(S["l_ready"], t + 1)
                    pe.wait_ge(S["bs_ready"], q + 1)
                    mm(b_ps[n % 2][:, :], state_sel[:, n:n + 1].broadcast_to([C, C]), hl[r][:, :]).then_inc(S["bbc_ready"], 1)

                def bcast_c(t, r, n):
                    q = DS * t + n
                    pe.wait_ge(S["prod_ready"], q + 1)
                    mm(c_ps[n % 2][:, :], state_sel[:, DS + n:DS + n + 1].broadcast_to([C, C]), hl[r][:, :]).then_inc(S["cbc_ready"], 1)

                def skip_u(t, r, seen):
                    if seen:
                        pe.wait_ge(S["y_ready"], t)
                    for h in range(HALVES):
                        mm(y_ps[h][:, :], w_skip[:, h, :], u[r][:, h, :], stop=False)

                def sum_y(t, n):
                    q = DS * t + n
                    pe.wait_ge(S["prod_ready"], q + 1 + RING)
                    for h in range(HALVES):
                        m = mm(y_ps[h][:, :], ident, prod[n % DEEP][:, h, :], start=False, stop=(n == DS - 1))
                    m.then_inc(S["prod_used"], 1)

                t0 = TILES * b
                for step in range(DS):
                    front(t0, step, first=True)
                for step in range(DS):
                    back(t0, 0, step)
                    front(t0 + 1, step)
                for n in range(LEAD + 2):
                    bcast_b(t0, 0, n)
                bcast_c(t0, 0, 0)

                def tile0(i, p, seen, left):
                    t = TILES * b + i
                    for n in range(DS):
                        ahead = n + LEAD + 2
                        if ahead < DS:
                            bcast_b(t, p, ahead)
                        elif left:
                            bcast_b(t + 1, 1 - p, ahead - DS)
                        if n + 1 < DS:
                            bcast_c(t, p, n + 1)
                        elif left:
                            bcast_c(t + 1, 1 - p, 0)
                        if seen and n == 0:
                            sum_y(t - 1, DS - 1)
                        if n == 1:
                            skip_u(t, p, seen)
                        if n >= 1:
                            sum_y(t, n - 1)
                        if left:
                            back(t + 1, 1 - p, n, seen)
                        if n == 5 and seen:
                            post(t - 1, left)
                        if left == 2:
                            front(t + 2, n)
                pairs(pe, tile0)
                sum_y(t0 + TILES - 1, DS - 1)
                pe.wait_ge(S["x0_upd"], t0 + TILES - 1)
                post(t0 + TILES - 1, 0)

                group_norm(1)

                def by_columns(t, p, ky):
                    if ky == 0:
                        pe.wait_ge(S["win1"], t + 1)
                    m = mm(bank[2][:, :].rearrange("p (r w) -> p r w", r=ROWS), w_kg[:, ky, :],
                           win[p][:, ky:ky + ROWS, 1:W + 1], start=(ky == 0), stop=(ky == 2))
                    if ky == 2:
                        m.then_inc(S["bycol_ps"], 1)

                def join_columns(t, kx):
                    if kx == 0:
                        pe.wait_ge(S["bycol_ready"], t + 1)
                    m = mm(bank[3][:, :].rearrange("p (r w) -> p r w", r=ROWS), shift_sel[:, kx, :],
                           by_column[:, :, kx:kx + W], start=(kx == 0), stop=(kx == 2))
                    if kx == 2:
                        m.then_inc(S["kern_ready"], 1)

                def pointwise(t, p):
                    pe.wait_ge(S["x1_upd"], t + 1)
                    mm(bank[p][:, :], w_pw[:, :], prods[p][:, TAPS - 1, :], stop=False)
                    pe.wait_ge(S["sump_ready"], t + 1)
                    mm(bank[p][:, :], w_pw[:, :], prods[p][:, 0, :], start=False).then_inc(S["pw_ready"], 1)

                for ky in range(3):
                    by_columns(t0, 0, ky)
                for kx in range(3):
                    join_columns(t0, kx)

                def tile1(i, p, seen, left):
                    t = TILES * b + i
                    for k in range(TAPS):
                        if k == 0:
                            pe.wait_ge(S["kl_ready"], t + 1)
                        pe.wait_ge(S["prod1_ready"], TAPS * t + k + 1)
                        mm(bank[4 + k % BC_BANKS][:, :], tap_sel[:, k, :], hl[p][:, :]).then_inc(S["bc_ready"], 1)
                        if left and 2 <= k < 5:
                            by_columns(t + 1, 1 - p, k - 2)
                        if left and k >= 6:
                            join_columns(t + 1, k - 6)
                    if seen:
                        pointwise(t - 1, 1 - p)
                pairs(pe, tile1)
                pe.wait_ge(S["prod1_ready"], TAPS * (t0 + TILES) + BC_BANKS)
                pointwise(t0 + TILES - 1, 1)

                group_norm(2)
                pe.wait_ge(S["late_in"], 16 * 9 * (b + 1))
                pe.wait_ge(S["avg_ready"], b + 1)
                mm(work0[:, 0:1], se_w1, avg).then_inc(S["se1_ps"], 1)
                pe.wait_ge(S["se1_ready"], b + 1)
                mm(work1[:, 0:1], se_w2, se_mid).then_inc(S["se2_ps"], 1)

                def conv(dst, p, stop):
                    for k in range(TAPS):
                        for w_part, x_part in ((0, 0), (0, 1), (1, 0)):
                            m = mm(dst[:, :].rearrange("p (r w) -> p r w", r=ROWS), w_hl[w_part][:, k, :],
                                   win_hl[p][x_part][:, k // 3:k // 3 + ROWS, k % 3:k % 3 + W],
                                   start=(k == 0 and w_part == x_part), stop=(stop and k == TAPS - 1 and w_part == 1))
                    return m

                pe.wait_ge(S["w_split"], 2 * b + 1)

                def tile2(i, p, seen, left):
                    t = TILES * b + i
                    pe.wait_ge(S["split2"], t + 1)
                    if seen == 2:
                        pe.wait_ge(S["gated_ready"], t - 1)
                    conv(bank[2 + p], p, True).then_inc(S["conv2_ready"], 1)
                pairs(pe, tile2)

                group_norm(3)

                def spectrum(i, p, seen, left):
                    t = TILES * b + i
                    pe.wait_ge(S["g3_ready"], t + 1)
                    if seen == 2:
                        pe.wait_ge(S["rowt_ready"], t - 1)
                    for r in range(ROWS):
                        m = pe.transpose(bank[2 + p][:, W * r:W * (r + 1)], g_norm[p][:, W * r:W * (r + 1)], ident)
                    m.then_inc(S["rowt_ps"], 1)
                    if seen:
                        dft_rows(t - 1, 1 - p)
                    if not left:
                        dft_rows(t, p)

                def dft_rows(t, p):
                    pe.wait_ge(S["rowt_ready"], t + 1)
                    pe.wait_ge(S["dftw_ready"], t + 1)
                    for r in range(ROWS):
                        m = mm(bank[4 + p][:, 32 * r:32 * (r + 1)], row_t[p][:, W * r:W * (r + 1)], fw)
                    m.then_inc(S["dftw_ps"], 1)
                pairs(pe, spectrum)
                pe.wait_ge(S["dftw_ready"], t0 + TILES + RING)
                for j in range(8):
                    if j >= 2:
                        pe.wait_ge(S["dftt_ready"], 8 * b + j - 1)
                    for f in range(4):
                        m = pe.transpose(bank[2 + j % 2][:, C * f:C * (f + 1)], dft_w[:, :, 4 * j + f], ident)
                    m.then_inc(S["dftt_ps"], 1)
                pe.wait_ge(S["dftt_ready"], 8 * (b + 1))
                for fy in range(MODES):
                    mm(work0[:, 32 * fy:32 * (fy + 1)], dft_wt[:, 2 * fy, :], fh[:, 0:32], stop=False)
                    m = mm(work0[:, 32 * fy:32 * (fy + 1)], dft_wt[:, 2 * fy + 1, :], fh[:, 32:64], start=False)
                m.then_inc(S["spec_ps"], 1)

                def conv3(t, p):
                    pe.wait_ge(S["split3"], t + 1)
                    conv(bank[4 + p], p, False)

                pe.wait_ge(S["w_split"], 2 * b + 2)

                conv3(t0, 0)
                conv3(t0 + 1, 1)
                for k in range(TAPS):
                    pe.wait_ge(S["xt_ready"], TAPS * b + k + 1)
                    for j in range(4):
                        m = mm(o_ps[j][:, 0:C], x_tap[:, k, C * j:C * (j + 1)], w3[:, k, :],
                               start=(k == 0), stop=(k == TAPS - 1))
                m.then_inc(S["o_ps"], 1)

                def low_rows(t, p):
                    pe.wait_ge(S["ta_ready"], t + 1)
                    for j in range(4):
                        m = mm(bank[6 + p][32 * j:32 * (j + 1), 0:C], ta[p], o_t[:, j, :])
                    m.then_inc(S["low_ps"], 1)

                pe.wait_ge(S["o_ready"], b + 1)
                low_rows(t0, 0)

                def tile3(i, p, seen, left):
                    t = TILES * b + i
                    if seen == 2:
                        pe.wait_ge(S["out_ready"], t - 1)
                        conv3(t, p)
                    if left:
                        low_rows(t + 1, 1 - p)
                    pe.wait_ge(S["low_ready"], t + 1)
                    mm(bank[4 + p][:, :], low[p], tab_b, start=False).then_inc(S["conv3_ready"], 1)
                pairs(pe, tile3)

        @block.scalar
        def _(act):
            act.preload_act_table_set(LN_EXP)
            act.wait_ge(S["weights_in"], loaded)
            act.activation(a_neg[:, :, :], a_neg[:, :, :], ACT.Exp).then_inc(S["prep_act"], 1)

            with act.Fori(0, BATCH) as b:
                def group_norm(layer):
                    s = 4 * b + layer + 1
                    act.wait_ge(S["gvar_ps"], s)
                    act.activation(glog, work1[:, 0:1], ACT.Ln, bias=eps_gn).then_inc(S["glog_ready"], 1)
                    act.wait_ge(S["glog_ready"], s)
                    act.activation(grstd, glog, ACT.Exp, scale=-0.5).then_inc(S["grstd_ready"], 1)

                act.preload_act_table_set(LN_EXP)
                group_norm(0)

                def front(t, i, step, first=False):
                    if step == 10:
                        if first:
                            act.wait_ge(S["gshift_ready"], b + 1)
                        else:
                            act.wait_ge(S["u_ready"], t)
                        act.activation(g_tile, px(i), ACT.Identity, scale=grstd, bias=gshift).then_inc(S["g_ready"], 1)
                    if step == 12:
                        act.wait_ge(S["cen_ready"], t + 1)
                        act.activation(sq, work1[:, :], ACT.Square).then_inc(S["sq_ready"], 1)
                    if step == 14:
                        act.wait_ge(S["var_ready"], t + 1)
                        act.activation(rs, work0[:, :], ACT.Ln, bias=eps_gn).then_inc(S["lnv_ready"], 1)
                        act.wait_ge(S["lnv_ready"], t + 1)
                        act.activation(rs, rs, ACT.Exp, scale=-0.5).then_inc(S["rs_ready"], 1)

                def back(t, r, step, seen=0, start=False):
                    if step == 1:
                        if start:
                            prev = zero3.rearrange("p (h t) -> p h t", h=HALVES)
                        else:
                            act.wait_ge(S["tap_done"], 6 * t)
                            prev = xin[:, :, T:T + 3]
                        act.activation(xin[:, :, 0:3], prev, ACT.Copy).then_inc(S["hist_done"], 1)
                        act.wait_ge(S["hist_done"], t + 1)
                        for h in range(HALVES):
                            act.wait_ge(S["xin_ready"], 2 * t + h + 1)
                            src = (work0, work1)[h]
                            act.activation(xin[:, h, 3:T + 3], src[:, :], ACT.Identity, bias=bias_in[:, h:h + 1])
                            act.activation(u[r][:, h, :], src[:, :], ACT.Identity, scale=conv_w[:, h, 3:4],
                                           bias=conv_b3[:, h:h + 1]).then_inc(S["xin_evac"], 1)
                    if step in (3, 4):
                        h = step - 3
                        if h == 0:
                            act.preload_act_table_set(EXP_TANH)
                            if seen:
                                act.wait_ge(S["yz_ready"], t - 1)
                        act.wait_ge(S["z_ready"], 2 * t + h + 1)
                        src = (work0, work1)[h]
                        act.activation(zs[r][:, h, :], src[:, :], ACT.Identity, bias=bias_in[:, 2 + h:3 + h])
                        act.activation(tmp_z[:, h, :], src[:, :], ACT.Tanh,
                                       bias=bias_in[:, 2 + h:3 + h]).then_inc(S["z_evac"], 1)
                    if step == 4:
                        act.wait_ge(S["tap_done"], 6 * (t + 1))
                        act.activation(tmp_u, u[r], ACT.Tanh).then_inc(S["thu_ready"], 1)
                        act.preload_act_table_set(LN_EXP)
                    if step == 7:
                        act.wait_ge(S["xdbl_ready"], t + 1)
                        act.activation(dts, work0[:, :], ACT.Copy).then_inc(S["dts_ready"], 1)
                        act.activation(hl[r][:, :], work0[:, :], ACT.Copy).then_inc(S["hh_ready"], 1)
                    if step == 9:
                        act.wait_ge(S["zs_ready"], t + 1)
                        for h in range(HALVES):
                            act.wait_ge(S["dt_ready"], 2 * t + h + 1)
                            v = (work1, work0)[h]
                            act.activation(tmp_z[:, h, :], v[:, :], ACT.Abs, bias=dt_b[:, h:h + 1])
                            act.activation(delta[r][:, h, :], v[:, :], ACT.Relu,
                                           bias=dt_b[:, h:h + 1]).then_inc(S["v_done"], 1)
                    if step == 10:
                        act.wait_ge(S["v_done"], 2 * t + 2)
                        act.activation(tmp_z, tmp_z, ACT.Exp, scale=-1.0).then_inc(S["exp_done"], 1)
                        act.wait_ge(S["exp_done"], t + 1)
                        act.activation(tmp_z, tmp_z, ACT.Ln, bias=1.0).then_inc(S["sp_ready"], 1)

                def copy_y(t, seen):
                    act.wait_ge(S["prod_used"], DS * (t + 1) + DEEP)
                    if seen:
                        act.wait_ge(S["proj_ready"], t)
                    for h in range(HALVES):
                        a = act.activation(yd[:, h, :], y_ps[h][:, :], ACT.Copy)
                    a.then_inc(S["y_ready"], 1)

                def copy_b(t, n):
                    q = DS * t + n
                    act.wait_ge(S["bbc_ready"], q + 1)
                    act.wait_ge(S["dbu_ready"], q + 1)
                    act.activation(b_sb[n % DEEP], b_ps[n % 2][:, :], ACT.Copy).then_inc(S["bs_ready"], 1)

                def decay(t, r, n, start=False):
                    q = DS * t + n
                    if n == 0:
                        act.wait_ge(S["delta_ready"], t + 1)
                    act.wait_ge(S["scan_ready"], q + 1)
                    if not start:
                        act.wait_ge(S["st_saved"], q - DS + 1 + DEEP)
                    act.activation(dBu[n % DEEP][:, :, 0:1], state[:, :, n:n + 1], ACT.Copy)
                    for h in range(HALVES):
                        a = act.activation(dA[n % DEEP][:, h, 1:1 + T], delta[r][:, h, :], ACT.Exp,
                                           scale=a_neg[:, h, n:n + 1])
                    a.then_inc(S["da_ready"], 1)

                t0 = TILES * b
                act.wait_ge(S["prep_dve"], 4)
                for step in range(DS):
                    front(t0, 0, step, first=True)
                for step in range(DS):
                    back(t0, 0, step, start=True)
                    front(t0 + 1, 1, step)
                for n in range(LEAD):
                    copy_b(t0, n)
                    decay(t0, 0, n, start=True)
                copy_b(t0, LEAD)

                def tile0(i, p, seen, left):
                    t = TILES * b + i
                    for n in range(DS):
                        ahead = n + LEAD
                        if ahead + 1 < DS:
                            copy_b(t, ahead + 1)
                        elif left:
                            copy_b(t + 1, ahead + 1 - DS)
                        if ahead < DS:
                            decay(t, p, ahead, start=not seen)
                        elif left:
                            decay(t + 1, 1 - p, ahead - DS)
                        if n == 0 and seen:
                            copy_y(t - 1, seen == 2)
                        if left:
                            back(t + 1, 1 - p, n, seen)
                        if left == 2:
                            front(t + 2, i + 2, n)
                pairs(act, tile0)
                copy_y(t0 + TILES - 1, True)

                group_norm(1)

                def head(t, p):
                    act.wait_ge(S["bycol_ps"], t + 1)
                    act.activation(by_column[:, :, 1:W + 1], bank[2][:, :].rearrange("p (r w) -> p r w", r=ROWS),
                                   ACT.Copy).then_inc(S["bycol_ready"], 1)
                    act.wait_ge(S["kern_ready"], t + 1)
                    act.activation(hl[p][:, :], bank[3][:, :], ACT.Identity, bias=b_kg).then_inc(S["kh_ready"], 1)

                head(t0, 0)

                def tile1(i, p, seen, left):
                    if left:
                        head(TILES * b + i + 1, 1 - p)
                pairs(act, tile1)

                def round_weights(w):
                    act.activation(w_hl[0][:, :, :], w, ACT.Copy).then_inc(S["w_rounded"], 1)

                def round_window(t, p, layer):
                    act.wait_ge(S[f"win{layer}"], t + 1)
                    act.activation(win_hl[p][0][:, :, :], win[p], ACT.Copy).then_inc(S[f"rounded{layer}"], 1)

                act.wait_ge(S["late_in"], 16 * 9 * (b + 1))
                act.wait_ge(S["bc_ready"], TAPS * (t0 + TILES))
                round_weights(w2)
                group_norm(2)
                act.wait_ge(S["se1_ps"], b + 1)
                act.activation(se_mid, work0[:, 0:1], ACT.Relu).then_inc(S["se1_ready"], 1)
                act.wait_ge(S["se2_ps"], b + 1)
                act.activation(se_exp, work1[:, 0:1], ACT.Exp, scale=-1.0).then_inc(S["seexp_ready"], 1)
                act.wait_ge(S["seb_ready"], b + 1)
                round_window(t0, 0, 2)

                def tile2(i, p, seen, left):
                    t = TILES * b + i
                    if left:
                        if seen:
                            act.wait_ge(S["conv2_ready"], t)
                        round_window(t + 1, 1 - p, 2)
                    act.wait_ge(S["conv2_ready"], t + 1)
                    if seen == 2:
                        act.wait_ge(S["x2_upd"], t - 1)
                    act.activation(gated[p], bank[2 + p][:, :], ACT.Identity, scale=se,
                                   bias=se_b).then_inc(S["gated_ready"], 1)
                pairs(act, tile2)

                group_norm(3)

                def spectrum(i, p, seen, left):
                    t = TILES * b + i
                    act.wait_ge(S["rowt_ps"], t + 1)
                    if seen == 2:
                        act.wait_ge(S["dftw_ps"], t - 1)
                    act.activation(row_t[p], bank[2 + p][:, :], ACT.Copy).then_inc(S["rowt_ready"], 1)
                pairs(act, spectrum)
                round_weights(w3)
                for j in range(8):
                    act.wait_ge(S["dftt_ps"], 8 * b + j + 1)
                    act.activation(dft_wt[:, 4 * j:4 * (j + 1), :],
                                   bank[2 + j % 2][:, :].rearrange("p (f c) -> p f c", f=4),
                                   ACT.Copy).then_inc(S["dftt_ready"], 1)
                for p in range(2):
                    round_window(t0 + p, p, 3)
                act.wait_ge(S["o_ps"], b + 1)
                for j in range(4):
                    a = act.activation(o_t[:, j, :], o_ps[j][:, 0:C], ACT.Copy)
                a.then_inc(S["o_ready"], 1)

                def tile3(i, p, seen, left):
                    t = TILES * b + i
                    act.wait_ge(S["low_ps"], t + 1)
                    if seen == 2:
                        act.wait_ge(S["conv3_ready"], t - 1)
                    act.activation(low[p], bank[6 + p][:, 0:C], ACT.Copy).then_inc(S["low_ready"], 1)
                    if left and seen:
                        act.wait_ge(S["conv3_ready"], t)
                        round_window(t + 1, 1 - p, 3)
                pairs(act, tile3)

        @block.gpsimd
        def _(pool):
            for m in (w_x[:, :, :], w_dt[:, :, :], w_kg[:, :, :], w_pw[:, :]):
                pool.memset(m, 0.0).then_inc(S["prep_pool"], 1)
            pool.memset(ones[:, :], 1.0)
            pool.memset(cols[:, :], 0.0).then_inc(S["prep_pool"], 1)

            with pool.Fori(0, BATCH) as b:
                def input_gain(t, r, start=False):
                    pool.wait_ge(S["delta_ready"], t + 1)
                    if not start:
                        pool.wait_ge(S["dbu_ready"], DS * t + DEEP)
                    pool.tensor_tensor(du, delta[r], u[r], ALU.mult).then_inc(S["du_ready"], 1)

                def drive(t, n):
                    q = DS * t + n
                    if n == 0:
                        pool.wait_ge(S["du_ready"], t + 1)
                    pool.wait_ge(S["bs_ready"], q + 1 + RING)
                    pool.wait_ge(S["scan_ready"], q + 1)
                    pool.tensor_tensor(dBu[n % DEEP][:, :, 1:1 + T], du, b_sb[n % DEEP].unsqueeze(1).broadcast_to([C, HALVES, T]),
                                       ALU.mult).then_inc(S["dbu_ready"], 1)

                def save(t, n):
                    pool.wait_ge(S["scan_ready"], DS * t + n + 1 + DEEP)
                    pool.tensor_tensor(state[:, :, n:n + 1], hst[n % DEEP][:, :, T:1 + T], ones2,
                                       ALU.mult).then_inc(S["st_saved"], 1)

                def gate(t, r):
                    pool.wait_ge(S["y_ready"], t + 1)
                    pool.wait_ge(S["zs_ready"], t + 1)
                    pool.tensor_tensor(yd, yd, zs[r], ALU.mult).then_inc(S["yz_ready"], 1)

                t0 = TILES * b
                input_gain(t0, 0, start=True)
                for n in range(LEAD):
                    drive(t0, n)

                def tile0(i, p, seen, left):
                    t = TILES * b + i
                    for n in range(DS):
                        ahead = n + LEAD
                        save(t, n)
                        if left and ahead == DS:
                            input_gain(t + 1, 1 - p)
                        if ahead < DS:
                            drive(t, ahead)
                        elif left:
                            drive(t + 1, ahead - DS)
                        if n == 1 and seen:
                            gate(t - 1, 1 - p)
                pairs(pool, tile0)
                gate(t0 + TILES - 1, 1)

                def tile1(i, p, seen, left):
                    t = TILES * b + i
                    pr = prods[p]
                    for half in range(2):
                        pool.wait_ge(S["prod1_ready"], TAPS * t + 4 * (half + 1) + BC_BANKS)
                        lo = 4 * half
                        pool.tensor_tensor(pr[:, lo:lo + 2, :], pr[:, lo:lo + 2, :], pr[:, lo + 2:lo + 4, :],
                                           ALU.add).then_inc(S["addp_done"], 1)
                    pool.wait_ge(S["addp_done"], 3 * t + 2)
                    pool.tensor_tensor(pr[:, 0:2, :], pr[:, 0:2, :], pr[:, 4:6, :],
                                       ALU.add).then_inc(S["addp_done"], 1)
                    pool.wait_ge(S["addp_done"], 3 * t + 3)
                    pool.tensor_tensor(pr[:, 0, :], pr[:, 0, :], pr[:, 1, :], ALU.add).then_inc(S["sump_ready"], 1)
                pairs(pool, tile1)

                pool.wait_ge(S["late_in"], 16 * 9 * (b + 1))
                pool.wait_ge(S["o_ready"], b + 1)

                def tile3(i, p, seen, left):
                    t = TILES * b + i
                    if seen == 2:
                        pool.wait_ge(S["low_ps"], t - 1)
                    pool.tensor_tensor(ta[p], tab_a[:, ds(32 * i, 32)], ones[:, 0:1].broadcast_to([C, 32]),
                                       ALU.mult).then_inc(S["ta_ready"], 1)
                pairs(pool, tile3)

        @block.vector
        def _(dve):
            done = S["prep_dve"]
            dve.wait_ge(S["weights_in"], loaded)
            dve.wait_ge(S["prep_pe"], 1)
            dve.tensor_copy(state_sel[:, :], arena[:, C:C + 2 * DS])
            dve.memset(eps_gn, 1e-5)
            for h in range(HALVES):
                dve.tensor_scalar(w_skip[:, h, :], ident, d_skip[:, h:h + 1], None, ALU.mult)
            dve.tensor_scalar(w_in[:, 0:2 * C], w_in[:, 0:2 * C], ln_w, None, ALU.mult)
            dve.tensor_scalar(w_in[:, 2 * C:4 * C], w_in[:, 2 * C:4 * C], ln_w, 0.5, ALU.mult, ALU.mult)
            dve.tensor_scalar(bias_in[:, 0:2], work0[:, 0:2], 1.0, None, ALU.mult)
            dve.tensor_scalar(bias_in[:, 2:4], work0[:, 2:4], 0.5, None, ALU.mult)
            dve.tensor_tensor(b_l3, b_l3, b_one, ALU.add)
            dve.tensor_scalar(conv_b, conv_b, 0.5, None, ALU.mult)
            dve.tensor_scalar(conv_w[:, :, :], conv_w[:, :, :], 0.5, None, ALU.mult).then_inc(done, 1)
            dve.wait_ge(done, 1)
            dve.tensor_tensor(conv_b3, conv_w[:, :, 3:4].squeeze(2), bias_in[:, 0:2], ALU.mult).then_inc(done, 1)
            dve.wait_ge(done, 2)
            dve.tensor_tensor(conv_b3, conv_b3, conv_b, ALU.add).then_inc(done, 1)
            dve.wait_ge(S["prep_act"], 1)
            dve.tensor_scalar(a_neg[:, :, :], a_neg[:, :, :], -1.0, None, ALU.mult).then_inc(done, 1)
            dve.wait_ge(done, 4)

            def tile_stats(i):
                dve.bn_stats(stats[:, ds(i, 1), :].rearrange("p a s -> p (a s)"), px(i)).then_inc(S["stats_done"], 1)

            for k in range(8):
                dve.wait_ge(x_first[k], 16)
                for j in range(4):
                    tile_stats(4 * k + j)

            with dve.Fori(0, BATCH) as b:
                def group_norm(layer):
                    s = 4 * b + layer + 1
                    dve.wait_ge(S["stats_done"], TILES * s)
                    dve.memset(spare, 0.0)
                    dve.bn_aggr(mv, stats[:, :, :].rearrange("p t s -> p (t s)")).then_inc(S["mv_ready"], 1)
                    dve.wait_ge(S["mv_ready"], s)
                    dve.wait_ge(S["gmean_ps"], s)
                    dve.tensor_copy(gmean, work0[:, 0:1]).then_inc(S["gmean_ready"], 1)
                    dve.wait_ge(S["gmean_ready"], 2 * s - 1)
                    dve.tensor_tensor(dmean, mv[:, 0:1], gmean, ALU.subtract).then_inc(S["gmean_ready"], 1)
                    dve.wait_ge(S["gmean_ready"], 2 * s)
                    dve.scalar_tensor_tensor(out=gvar, in0=dmean, scalar=dmean, in1=mv[:, 1:2], op0=ALU.mult,
                                             op1=ALU.add).then_inc(S["gvar_ready"], 1)
                    dve.wait_ge(S["grstd_ready"], s)

                def normalise(dst, src):
                    return dve.tensor_scalar(dst, src, gmean, grstd, ALU.subtract, ALU.mult)

                def window(i, p, counter):
                    normalise(win[p][:, :, 1:W + 1],
                              px(i, 6, 1).rearrange("p (r w) -> p r w", r=6)).then_inc(S[counter], 1)

                def pad_rows(layer):
                    for r in (0, H + 1):
                        dve.tensor_scalar(xres[:, W * r:W * (r + 1)], ident, 0.0, gmean, ALU.mult,
                                          ALU.add).then_inc(S["pads_done"], 1)
                    dve.wait_ge(S["pads_done"], 6 * b + 2 * layer)

                for p in range(2):
                    dve.wait_ge(stored[p], 16 * (TILES // 2) * b + 16)

                group_norm(0)

                def taps(t, r, k):
                    for h in range(HALVES):
                        if k < 2:
                            dve.wait_ge(S["tap_done"], 6 * t + 2 * (2 - k) - 1 + h)
                        dve.scalar_tensor_tensor(out=u[r][:, h, :], in0=xin[:, h, k:k + T],
                                                 scalar=conv_w[:, h, k:k + 1], in1=u[r][:, h, :],
                                                 op0=ALU.mult, op1=ALU.add).then_inc(S["tap_done"], 1)

                def front(t, step):
                    if step == 15:
                        dve.wait_ge(S["rs_ready"], t + 1)
                        dve.tensor_tensor(xn, work1[:, :], rs, ALU.mult).then_inc(S["xn_ready"], 1)

                def back(t, r, step):
                    if step == 2:
                        dve.wait_ge(S["xin_evac"], 2 * t + 2)
                        taps(t, r, 2)
                    if step == 3:
                        taps(t, r, 1)
                        taps(t, r, 0)
                    if step == 5:
                        dve.wait_ge(S["thu_ready"], t + 1)
                        dve.scalar_tensor_tensor(out=u[r], in0=tmp_u, scalar=1.0, in1=u[r], op0=ALU.add,
                                                 op1=ALU.mult).then_inc(S["u_ready"], 1)
                    if step == 6:
                        dve.wait_ge(S["z_evac"], 2 * t + 2)
                        dve.scalar_tensor_tensor(out=zs[r], in0=tmp_z, scalar=1.0, in1=zs[r], op0=ALU.add,
                                                 op1=ALU.mult).then_inc(S["zs_ready"], 1)
                    if step == 8:
                        dve.wait_ge(S["hh_ready"], t + 1)
                        dve.tensor_tensor(hl[r][64:96, :], dts[64:96, :], hl[r][64:96, :].bitcast(F32),
                                          ALU.subtract).then_inc(S["l_ready"], 1)

                def step_size(t, r, step):
                    if step == 11:
                        dve.wait_ge(S["sp_ready"], t + 1)
                        dve.tensor_tensor(delta[r], delta[r], tmp_z, ALU.add).then_inc(S["delta_ready"], 1)

                def post(t, i, r, step):
                    if step == 6:
                        dve.wait_ge(S["proj_ready"], t + 1)
                        dve.tensor_tensor(px(i), work1[:, :], px(i), ALU.add).then_inc(S["x0_upd"], 1)
                    if step == 8:
                        dve.wait_ge(S["x0_upd"], t + 1)
                        tile_stats(i)

                def scan(t, n, first=False):
                    q = DS * t + n
                    dve.wait_ge(S["da_ready"], q + 1)
                    dve.wait_ge(S["dbu_ready"], q + 1 + DEEP)
                    dve.wait_ge(S["st_saved"], q + 1)
                    if not first:
                        dve.wait_ge(S["prod_ready"], q - 1)
                    decays, drives, states = (v[n % DEEP].rearrange("p h t -> p (h t)") for v in (dA, dBu, hst))
                    dve.tensor_tensor_scan(states, decays, drives, 0.0, ALU.mult, ALU.add).then_inc(S["scan_ready"], 1)

                def read_out(t, n):
                    q = DS * t + n
                    dve.wait_ge(S["scan_ready"], q + 1 + DEEP)
                    dve.wait_ge(S["cbc_ready"], q + 1)
                    dve.wait_ge(S["prod_used"], q + 1)
                    dve.tensor_tensor(prod[n % DEEP], hst[n % DEEP][:, :, 1:1 + T], c_ps[n % 2][:, :].unsqueeze(1).broadcast_to(
                        [C, HALVES, T]), ALU.mult).then_inc(S["prod_ready"], 1)

                t0 = TILES * b
                dve.scalar_tensor_tensor(out=gshift, in0=gmean, scalar=-1.0, in1=grstd, op0=ALU.mult,
                                         op1=ALU.mult)
                dve.memset(state[:, :, :], 0.0)
                for k in range(DEEP):
                    a = dve.memset(dA[k][:, :, 0:1], 0.0)
                a.then_inc(S["gshift_ready"], 1)
                for step in range(DS):
                    front(t0, step)
                for step in range(DS):
                    back(t0, 0, step)
                    step_size(t0, 0, step)
                    front(t0 + 1, step)
                scan(t0, 0, first=True)

                def tile0(i, p, seen, left):
                    t = TILES * b + i
                    for n in range(DS):
                        if n + 1 < DS:
                            scan(t, n + 1, first=not seen)
                        elif left:
                            scan(t + 1, 0)
                        read_out(t, n)
                        if left:
                            back(t + 1, 1 - p, n)
                            step_size(t + 1, 1 - p, n)
                        if seen:
                            post(t - 1, i - 1, 1 - p, n)
                        if left == 2:
                            front(t + 2, n)
                pairs(dve, tile0)
                for step in range(DS):
                    post(t0 + TILES - 1, TILES - 1, 1, step)

                group_norm(1)
                pad_rows(1)
                for p in range(2):
                    dve.memset(win[p][:, :, 0:1], 0.0)
                    dve.memset(win[p][:, :, W + 1:W + 2], 0.0)
                dve.memset(by_column[:, :, 0:1], 0.0)
                dve.memset(by_column[:, :, W + 1:W + 2], 0.0)

                def rest(t, p):
                    dve.wait_ge(S["kh_ready"], t + 1)
                    dve.scalar_tensor_tensor(out=hl[p][64:128, :], in0=bank[3][64:128, :],
                                             scalar=b_kg[64:128, :], in1=hl[p][64:128, :].bitcast(F32),
                                             op0=ALU.add, op1=ALU.subtract).then_inc(S["kl_ready"], 1)

                def update1(t, i, p):
                    dve.wait_ge(S["pw_ready"], t + 1)
                    dve.scalar_tensor_tensor(out=px(i), in0=bank[p][:, :], scalar=b_pw, in1=px(i),
                                             op0=ALU.add, op1=ALU.add).then_inc(S["x1_upd"], 1)

                def stats1(t, i):
                    dve.wait_ge(S["x1_upd"], t + 1 + RING)
                    tile_stats(i)

                window(0, 0, "win1")
                dve.tensor_copy(tap_sel[:, :, :].rearrange("p k (g m) -> p k g m", g=4),
                                kernel_sel[:, :].rearrange("p (g k) -> p k g", g=4).unsqueeze(3).broadcast_to(
                                    [C, TAPS, 4, C // 4])).then_inc(S["selectors"], 1)
                rest(t0, 0)

                def tile1(i, p, seen, left):
                    t = TILES * b + i
                    if left:
                        dve.wait_ge(S["prod1_ready"], TAPS * t + BC_BANKS)
                        window(i + 1, 1 - p, "win1")
                    if seen == 2:
                        dve.wait_ge(S["pw_ready"], t - 1)
                    for k in range(TAPS):
                        dve.wait_ge(S["bc_ready"], TAPS * t + k + 1)
                        dve.tensor_tensor(prods[p][:, k, :].rearrange("p (r w) -> p r w", r=ROWS),
                                          bank[4 + k % BC_BANKS][:, :].rearrange("p (r w) -> p r w", r=ROWS),
                                          win[p][:, k // 3:k // 3 + ROWS, k % 3:k % 3 + W],
                                          ALU.mult).then_inc(S["prod1_ready"], 1)
                        if k == 2 and seen == 2:
                            update1(t - 2, i - 2, p)
                        if k == 5 and seen == 2:
                            stats1(t - 2, i - 2)
                    if left:
                        rest(t + 1, 1 - p)
                pairs(dve, tile1)
                def split_weights(w, k):
                    dve.wait_ge(S["w_rounded"], 2 * b + k)
                    dve.tensor_tensor(w_hl[1][:, :, :], w, w_hl[0][:, :, :].bitcast(F32),
                                      ALU.subtract).then_inc(S["w_split"], 1)

                def split_window(t, p, layer):
                    dve.wait_ge(S[f"rounded{layer}"], t + 1)
                    dve.tensor_tensor(win_hl[p][1][:, :, :], win[p], win_hl[p][0][:, :, :].bitcast(F32),
                                      ALU.subtract).then_inc(S[f"split{layer}"], 1)

                split_weights(w2, 1)
                for back_to in (2, 1):
                    i = TILES - back_to
                    update1(t0 + i, i, i % 2)
                    stats1(t0 + i, i)

                group_norm(2)
                pad_rows(2)
                dve.tensor_tensor(avg, dmean, grstd, ALU.mult).then_inc(S["avg_ready"], 1)
                dve.wait_ge(S["seexp_ready"], b + 1)
                dve.tensor_scalar(se, se_exp, 1.0, None, ALU.add).then_inc(S["seadd_ready"], 1)
                dve.wait_ge(S["seadd_ready"], b + 1)
                dve.reciprocal(se, se).then_inc(S["se_ready"], 1)
                dve.wait_ge(S["se_ready"], b + 1)
                dve.tensor_tensor(se_b, b_e, se, ALU.mult).then_inc(S["seb_ready"], 1)

                def update2(t, i, p):
                    dve.wait_ge(S["gated_ready"], t + 1)
                    dve.tensor_tensor(px(i), gated[p], px(i), ALU.add).then_inc(S["x2_upd"], 1)
                    dve.wait_ge(S["x2_upd"], t + 1)
                    tile_stats(i)

                window(0, 0, "win2")
                window(1, 1, "win2")
                split_window(t0, 0, 2)

                def tile2(i, p, seen, left):
                    t = TILES * b + i
                    if left:
                        split_window(t + 1, 1 - p, 2)
                    if seen:
                        dve.wait_ge(S["win2"], t + (2 if left else 1))
                        update2(t - 1, i - 1, 1 - p)
                    if left == 2:
                        dve.wait_ge(S["split2"], t + 1)
                        window(i + 2, p, "win2")
                pairs(dve, tile2)
                update2(t0 + TILES - 1, TILES - 1, 1)

                group_norm(3)
                pad_rows(3)

                def spectrum(i, p, seen, left):
                    t = TILES * b + i
                    if left:
                        if seen:
                            dve.wait_ge(S["rowt_ps"], t)
                        normalise(g_norm[1 - p], px(i + 1)).then_inc(S["g3_ready"], 1)
                    if seen:
                        keep_rows(t - 1, i - 1, 1 - p)
                    if not left:
                        keep_rows(t, i, p)

                def keep_rows(t, i, p):
                    dve.wait_ge(S["dftw_ps"], t + 1)
                    dve.tensor_copy(dft_w[:, ds(ROWS * i, ROWS), :],
                                    bank[4 + p][:, 0:32 * ROWS].rearrange("p (h f) -> p h f", h=ROWS)
                                    ).then_inc(S["dftw_ready"], 1)
                normalise(g_norm[0], px(0)).then_inc(S["g3_ready"], 1)
                pairs(dve, spectrum)
                split_weights(w3, 2)
                window(0, 0, "win3")
                window(1, 1, "win3")
                split_window(t0, 0, 3)
                split_window(t0 + 1, 1, 3)
                dve.wait_ge(S["split3"], t0 + 1)
                window(2, 0, "win3")

                def rotate(dst, src, axis, k):
                    cos, sin = (rot[:, T * (2 * axis + a):T * (2 * axis + a + 1)] for a in range(2))
                    x4, s4, r4 = (v.rearrange("p (y r x) -> p y r x", y=MODES, r=2) for v in (src, sin, rot_tmp))
                    q = (TAPS - 1) * b + k
                    for r in range(2):
                        a = dve.tensor_tensor(r4[:, :, r, :], x4[:, :, 1 - r, :], s4[:, :, r, :], ALU.mult)
                    dve.tensor_tensor(dst, src, cos, ALU.mult).then_inc(S["rot1_done"], 1)
                    dve.wait_ge(S["rot1_done"], q)
                    dve.tensor_tensor(dst, dst, rot_tmp, ALU.add).then_inc(S["xt_ready"], 1)

                dve.wait_ge(S["spec_ps"], b + 1)
                dve.tensor_copy(x_tap[:, 0, :], work0[:, :]).then_inc(S["xt_ready"], 1)
                for k in range(1, TAPS):
                    axis, of = (1, k - 1) if k % 3 else (0, k - 3)
                    dve.wait_ge(S["xt_ready"], TAPS * b + k)
                    rotate(x_tap[:, k, :], x_tap[:, of, :], axis, k)

                def store_tile(t, i, p):
                    dve.wait_ge(S["conv3_ready"], t + 1)
                    dve.wait_ge(stored[p], 8 * (t - p) + 16)
                    dve.scalar_tensor_tensor(out=out_buf[p], in0=bank[4 + p][:, :], scalar=b_l3, in1=px(i),
                                             op0=ALU.add, op1=ALU.add).then_inc(S["out_ready"], 1)

                def next_stats(i, p):
                    dve.wait_ge(x_in[p], 8 * (TILES * b + i - p) + 32)
                    tile_stats(i)

                def tile3(i, p, seen, left):
                    t = TILES * b + i
                    if left and seen:
                        split_window(t + 1, 1 - p, 3)
                    if seen:
                        store_tile(t - 1, i - 1, 1 - p)
                    if left == 2 and seen:
                        dve.wait_ge(S["split3"], t + 1)
                        window(i + 2, p, "win3")
                    if seen == 2:
                        next_stats(i - 2, p)
                pairs(dve, tile3)
                store_tile(t0 + TILES - 1, TILES - 1, 1)
                next_stats(TILES - 2, 0)
                next_stats(TILES - 1, 1)


_SHAPE = (BATCH, C, H, W)


def kernel(**inputs):
    from concourse import bacc
    from concourse.bass_utils import run_bass_kernel_spmd

    x = {k: np.asarray(v) for k, v in inputs.items()}

    def halves(a):
        return a.reshape(HALVES, C, -1).transpose(1, 0, 2)

    def column(a):
        return a.reshape(-1, 1)

    def taps(a):
        return a.reshape(a.shape[0], a.shape[1], TAPS).transpose(1, 2, 0)

    arrays = {
        "x": x["x"].reshape(BATCH, C, H * W),
        "w_in": x["L0_conv_W_in"].T, "w_x": halves(x["L0_conv_W_xproj"].T),
        "w_dt": x["L0_conv_W_dt"].T.reshape(8, HALVES, C), "w_out": halves(x["L0_conv_W_out"].T),
        "a_log": halves(x["L0_conv_A_log"]), "conv_w": halves(x["L0_conv_conv_w"]),
        "ln_w": column(x["L0_conv_ln_w"]), "ln_b": column(x["L0_conv_ln_b"]),
        "conv_b": x["L0_conv_conv_b"].reshape(HALVES, C).T, "b_dt": x["L0_conv_b_dt"].reshape(HALVES, C).T,
        "d": x["L0_conv_D"].reshape(HALVES, C).T,
        "w_kg": x["L1_conv_w_kg"].reshape(4, TAPS, 32, 3, 3).transpose(0, 4, 2, 3, 1),
        "b_kg": column(x["L1_conv_b_kg"]), "w_pw": x["L1_conv_w_pw"].reshape(4, 32, 32).transpose(0, 2, 1),
        "b_pw": column(x["L1_conv_b_pw"]),
        "w2": taps(x["L2_conv_weight"][0]), "b_e": column(x["L2_conv_bias_e"][0]),
        "se_w1": np.pad(x["L2_conv_se_w1"].T, ((0, 0), (0, C - 16))),
        "se_w2": np.pad(x["L2_conv_se_w2"].T, ((0, C - 16), (0, 0))),
        "w3": taps(x["L3_conv_weight"]), "b_l3": column(x["L3_conv_conv_bias"]),
        "b_one": x["L3_conv_bias"].reshape(1, 1),
        **{k: v.astype(np.float32) for k, v in shape_tables().items()},
    }
    arrays = {f"in_{k}": np.ascontiguousarray(v) for k, v in arrays.items()}
    nc = bacc.Bacc("TRN2", target_bir_lowering=False, num_devices=1)
    io = {k[3:]: nc.dram_tensor(k, v.shape, F32, kind="ExternalInput").ap() for k, v in arrays.items()}
    out = nc.dram_tensor("out", (BATCH, C, H * W), F32, kind="ExternalOutput").ap()
    build(nc, io, out)
    done = run_bass_kernel_spmd(nc, [arrays], core_ids=[0])
    return done.results[0]["out"].reshape(_SHAPE)
```
